# Optimizing a Trainium2 kernel written in Bass

```python
import numpy as np
import jax
import jax.numpy as jnp

def _softmax(x, axis=-1):
    return jax.nn.softmax(x, axis=axis)

def _gelu(x):
    return jax.nn.gelu(x, approximate=True)

def _silu(x):
    return jax.nn.silu(x)

def _sigmoid(x):
    return jax.nn.sigmoid(x)

def _layernorm(x, axis=-1, eps=1e-05):
    m = jnp.mean(x, axis=axis, keepdims=True)
    v = jnp.var(x, axis=axis, keepdims=True)
    return (x - m) / jnp.sqrt(v + eps)

def _scatter_add(tgt, idx, src, axis=0):
    return tgt.at[idx].add(src)

def _segment_sum(src, seg, n):
    return jax.ops.segment_sum(src, seg, n)
kernel_name = 'mk_gnn_resnorm_d1_gnn_r32_072358'

def setup_inputs(seed: int=0):
    np.random.seed(seed)
    _w = jnp.asarray

    def _rec_inputs():
        import jax
        import jax.numpy as jnp
        _gk = jax.random.key(seed)
        x = -0.000202 + 1 * jax.random.normal(jax.random.fold_in(_gk, 1), (3125, 64), jnp.float32)
        src = jax.random.randint(jax.random.fold_in(_gk, 2), (100000,), 0, 3125, jnp.int32)
        dst = jax.random.randint(jax.random.fold_in(_gk, 3), (100000,), 0, 3125, jnp.int32)
        _o = jnp.argsort(dst, stable=True)
        src = src[_o]
        dst = dst[_o]
        edge_attr_2 = jax.random.uniform(jax.random.fold_in(_gk, 11), (100000, 2), jnp.float32, 0.0, 1)
        return (x, src, dst, edge_attr_2)
    x, src, dst, edge_attr_2 = _rec_inputs()

    def _L0_gnn_setup():
        import jax, jax.numpy as jnp
        import numpy as np
        N_NODES = 3125
        N_EDGES = 50000
        IN_CH = 64
        OUT_CH = 64
        NUM_K = 9

        def _quad_basis(v):
            return jnp.stack([0.5 * v * v - v + 0.5, -v * v + v + 0.5, 0.5 * v * v], axis=-1)

        def spline_conv(x, src, dst, pseudo, W, root, bias, n_nodes):
            b0 = _quad_basis(pseudo[:, 0])
            b1 = _quad_basis(pseudo[:, 1])
            B = (b0[:, :, None] * b1[:, None, :]).reshape(pseudo.shape[0], NUM_K)
            x_src = x[src]
            msg = B[:, 0:1] * (x_src @ W[0])
            for k in range(1, NUM_K):
                msg = msg + B[:, k:k + 1] * (x_src @ W[k])
            out = jax.ops.segment_sum(msg, dst, num_segments=n_nodes)
            return out + x @ root + bias
        key = jax.random.key(seed)
        ks = jax.random.split(key, 10)
        x = jax.random.normal(ks[0], (N_NODES, IN_CH), dtype=jnp.float32)
        edge_index = jax.random.randint(ks[1], (2, N_EDGES), 0, N_NODES, dtype=jnp.int64)
        pseudo = jax.random.uniform(ks[2], (N_EDGES, 2), dtype=jnp.float32)
        s1 = 1.0 / np.sqrt(IN_CH * NUM_K)
        s2 = 1.0 / np.sqrt(OUT_CH * NUM_K)
        W1 = jax.random.normal(ks[3], (NUM_K, IN_CH, OUT_CH), dtype=jnp.float32) * s1
        root1 = jax.random.normal(ks[4], (IN_CH, OUT_CH), dtype=jnp.float32) * s1
        b1 = jax.random.normal(ks[5], (OUT_CH,), dtype=jnp.float32) * 0.01
        W2 = jax.random.normal(ks[6], (NUM_K, OUT_CH, OUT_CH), dtype=jnp.float32) * s2
        root2 = jax.random.normal(ks[7], (OUT_CH, OUT_CH), dtype=jnp.float32) * s2
        b2 = jax.random.normal(ks[8], (OUT_CH,), dtype=jnp.float32) * 0.01
        return {'x': x, 'edge_index': edge_index, 'pseudo': pseudo, 'W1': W1, 'root1': root1, 'b1': b1, 'W2': W2, 'root2': root2, 'b2': b2}
    _L0_gnn_all = _L0_gnn_setup()
    _L0_gnn_in = {k: v for k, v in _L0_gnn_all.items() if k in ('W1', 'root1', 'b1', 'W2', 'root2', 'b2')}
    del _L0_gnn_all
    return {'x': x, 'src': src, 'dst': dst, 'edge_attr_2': edge_attr_2, 'L0_gnn_W1': _L0_gnn_in['W1'], 'L0_gnn_root1': _L0_gnn_in['root1'], 'L0_gnn_b1': _L0_gnn_in['b1'], 'L0_gnn_W2': _L0_gnn_in['W2'], 'L0_gnn_root2': _L0_gnn_in['root2'], 'L0_gnn_b2': _L0_gnn_in['b2']}

def reference(x, src, dst, edge_attr_2, L0_gnn_W1, L0_gnn_root1, L0_gnn_b1, L0_gnn_W2, L0_gnn_root2, L0_gnn_b2):
    import jax
    import jax.numpy as jnp

    def _L0_gnn_ref(x, edge_index, pseudo, W1, root1, b1, W2, root2, b2):
        import jax, jax.numpy as jnp
        import numpy as np
        N_NODES = 3125
        N_EDGES = 50000
        IN_CH = 64
        OUT_CH = 64
        NUM_K = 9

        def _quad_basis(v):
            return jnp.stack([0.5 * v * v - v + 0.5, -v * v + v + 0.5, 0.5 * v * v], axis=-1)

        def spline_conv(x, src, dst, pseudo, W, root, bias, n_nodes):
            b0 = _quad_basis(pseudo[:, 0])
            b1 = _quad_basis(pseudo[:, 1])
            B = (b0[:, :, None] * b1[:, None, :]).reshape(pseudo.shape[0], NUM_K)
            x_src = x[src]
            msg = B[:, 0:1] * (x_src @ W[0])
            for k in range(1, NUM_K):
                msg = msg + B[:, k:k + 1] * (x_src @ W[k])
            out = jax.ops.segment_sum(msg, dst, num_segments=n_nodes)
            return out + x @ root + bias
        src, dst = (edge_index[0], edge_index[1])
        h = jax.nn.relu(spline_conv(x, src, dst, pseudo, W1, root1, b1, N_NODES))
        h = jax.nn.relu(spline_conv(h, src, dst, pseudo, W2, root2, b2, N_NODES))
        return h
    edge_index = jnp.stack([src, dst])
    x = _layernorm(x + _L0_gnn_ref(x, edge_index, edge_attr_2, L0_gnn_W1, L0_gnn_root1, L0_gnn_b1, L0_gnn_W2, L0_gnn_root2, L0_gnn_b2), axis=-1)
    return x

_drawn_inputs = setup_inputs


def setup_inputs(seed=0):
    import zlib

    import numpy as np

    out = dict(_drawn_inputs(seed))
    spreads = {}
    factors = {'L0_gnn_b1': 5.19, 'L0_gnn_b2': 8.0}
    for name, (base, spread) in spreads.items():
        noise = np.random.default_rng([zlib.crc32(name.encode()), seed]).standard_normal(out[name].shape)
        drawn = base * np.exp(spread * noise) if base else spread * noise
        out[name] = jnp.asarray(drawn.astype(out[name].dtype))
    for name, factor in factors.items():
        out[name] = (out[name] * factor).astype(out[name].dtype)
    return out
```

```python
import concourse.bass as bass
from concourse import mybir
from contextlib import ExitStack


def spline_gnn_program(nc, x, src, dst, attr, W1, root1, b1, W2, root2, b2, out):
    fp32 = mybir.dt.float32
    i32 = mybir.dt.int32
    ALU = mybir.AluOpType
    ACT = mybir.ActivationFunctionType
    AX = mybir.AxisListType.X
    DVE_ONLY = [mybir.EngineType.DVE]

    NODES, C = x.shape
    EDGES = src.shape[0]
    K = W1.shape[0]
    KH = (K + 1) // 2
    EPS = 1e-5

    P = 125
    T = EDGES // P
    U = 8
    LOOPS = T // (2 * U)
    NB = NODES // P
    ROWS = 100
    RG = T // ROWS
    W = 8
    WG = 100
    WINDOWS = -(-NODES // WG)
    NPAD = WINDOWS * WG
    FAR = 65536.0
    CB = 4
    CHUNKS = [(c, min(CB, NB - c)) for c in range(0, NB, CB)]
    LAYERS = [(W1, root1, b1), (W2, root2, b2)]
    assert T * P == EDGES and NB * P == NODES and LOOPS * 2 * U == T and RG * ROWS == T

    ctx = ExitStack()
    with ctx:
        def sb(name, shape, dt=fp32):
            return ctx.enter_context(nc.sbuf_tensor(name, shape, dt))

        def pb(name, shape):
            return ctx.enter_context(nc.psum_tensor(name, shape, fp32))

        def sem(name):
            return ctx.enter_context(nc.semaphore(name))

        h_dram = nc.dram_tensor("h_dram", (NODES, C), fp32, kind="Internal").ap()
        base_dram = nc.dram_tensor("base_dram", (T,), i32, kind="Internal").ap()

        src_i = sb("src_i", [ROWS, RG, P], i32)
        dst_i = sb("dst_i", [ROWS, RG, P], i32)
        attr_r = sb("attr_r", [ROWS, RG, P, 2])
        src_f = sb("src_f", [ROWS, RG, P])
        dst_f = sb("dst_f", [ROWS, RG, P])
        rel_f = sb("rel_f", [ROWS, RG, P])
        near_f = sb("near_f", [ROWS, RG, P])
        mark = sb("mark", [1, 1])
        base_f = sb("base_f", [ROWS, RG])
        base_i = sb("base_i", [ROWS, RG], i32)
        far_col = sb("far_col", [ROWS, 1])
        far_one = sb("far_one", [1, 1])
        flag_i = sb("flag_i", [1, 1], i32)
        base_row = sb("base_row", [1, T], i32)
        srcT = sb("srcT", [P, T])
        relT = sb("relT", [P, T])
        farT = sb("farT", [P, T])
        vT = sb("vT", [P, 2, T])
        quad = sb("quad", [P, 2, 3, T])
        basis = sb("basis", [P, T, 2 * KH])
        ident = sb("ident", [128, 128])
        iotaN = sb("iotaN", [P, NPAD], mybir.dt.int16)
        wst = [sb(f"wst{l}", [128, KH, C]) for l in range(2)]
        bias = [sb(f"bias{l}", [128, 1]) for l in range(2)]
        x_rows = sb("x_rows", [P, NB, C])
        h_rows = sb("h_rows", [P, NB, C])
        acc = sb("acc", [128, KH, NPAD])
        outT = sb("outT", [128, 2, CB * P])
        idx = sb("idx", [P, 2, U], i32)
        xg = sb("xg", [P, 2, U, C])
        hot = sb("hot", [P, 2, U, W])
        rhs = sb("rhs", [P, 2, U, 2 * KH, W])
        gen_idx = sb("gen_idx", [P, 1], i32)
        gen_x = sb("gen_x", [P, C])
        gen_hot = sb("gen_hot", [P, WG])
        gen_rhs = sb("gen_rhs", [P, 2 * KH, WG])
        ysum = sb("ysum", [P, NB])
        ysq = sb("ysq", [P, CB, C])
        yvar = sb("yvar", [P, NB])
        ystd = sb("ystd", [P, NB])
        yrstd = sb("yrstd", [P, NB])
        eps = sb("eps", [P, 1])

        ps_t = [pb(f"ps_t{i}", [128, 512]) for i in range(2)]
        ps_e = [pb(f"ps_e{i}", [128, 512]) for i in range(2)]
        ps_d = [pb(f"ps_d{i}", [128, 512]) for i in range(2)]
        ps_g = pb("ps_g", [128, 512])

        s_src = sem("s_src")
        s_dst = sem("s_dst")
        s_attr = sem("s_attr")
        s_x = sem("s_x")
        s_w = sem("s_w")
        s_const = sem("s_const")
        s_zero = sem("s_zero")
        s_rows = sem("s_rows")
        s_dve = sem("s_dve")
        s_tr = sem("s_tr")
        s_ev = [sem(f"s_ev{i}") for i in range(2)]
        s_base_w = sem("s_base_w")
        s_base_r = sem("s_base_r")
        s_far = sem("s_far")
        s_flagT = sem("s_flagT")
        s_flag = sem("s_flag")
        s_vT = sem("s_vT")
        s_basis = sem("s_basis")
        s_idx = [sem(f"s_idx{i}") for i in range(2)]
        s_gather = [sem(f"s_gather{i}") for i in range(2)]
        s_go = sem("s_go")
        s_hot = sem("s_hot")
        s_rhs = [sem(f"s_rhs{i}") for i in range(2)]
        s_mm = [sem(f"s_mm{i}") for i in range(2)]
        s_add = sem("s_add")
        s_acc = sem("s_acc")
        s_gi = [sem(f"s_gi{i}") for i in range(2)]
        s_gx = [sem(f"s_gx{i}") for i in range(2)]
        s_gh = [sem(f"s_gh{i}") for i in range(2)]
        s_gr = [sem(f"s_gr{i}") for i in range(2)]
        s_gm = [sem(f"s_gm{i}") for i in range(2)]
        s_ga = [sem(f"s_ga{i}") for i in range(2)]
        s_dense = sem("s_dense")
        s_relu = sem("s_relu")
        s_ht = sem("s_ht")
        s_hr = sem("s_hr")
        s_hd = sem("s_hd")
        s_clear = sem("s_clear")
        s_var = sem("s_var")
        s_std = sem("s_std")
        s_fin = sem("s_fin")
        s_out = sem("s_out")

        block = ctx.enter_context(nc.Block())

        rows_view = lambda a: a.rearrange("(r g p) -> r g p", r=ROWS, p=P)
        node_view = lambda a: a.rearrange("(j p) c -> p j c", p=P)
        HALF = RG // 2
        BATCHES = [(n, h) for n in ("src", "rel", "v0", "v1", "far") for h in range(2)] + \
                  [("x", c) for c in range(len(CHUNKS))]
        NBATCH = len(BATCHES)
        BASIS_READY = [sum(kind in ("v0", "v1") or n < 4 for n, (kind, _) in enumerate(BATCHES) if n % 2 == b)
                       for b in range(2)]

        @block.sync
        def _(sp):
            sp.dma_start(src_i[:], rows_view(src)).then_inc(s_src, 16)
            sp.dma_start(dst_i[:], rows_view(dst)).then_inc(s_dst, 16)
            sp.dma_start(attr_r[:], attr.rearrange("(r g p) v -> r g p v", r=ROWS, p=P)).then_inc(s_attr, 16)
            sp.dma_start(x_rows[:], node_view(x)).then_inc(s_x, 16)
            for l, (Wl, root, b) in enumerate(LAYERS):
                sp.dma_start(wst[l][0:C], Wl[0:KH].rearrange("k c o -> c k o")).then_inc(s_w, 16)
                sp.dma_start(wst[l][C:2 * C, 0:K - KH], Wl[KH:K].rearrange("k c o -> c k o")).then_inc(s_w, 16)
                sp.dma_start(wst[l][C:2 * C, K - KH], root).then_inc(s_w, 16)
                sp.dma_start(bias[l][C:2 * C, :], b.rearrange("(c o) -> c o", o=1)).then_inc(s_w, 16)
            sp.wait_ge(s_rows, 2)
            sp.dma_start(base_dram.rearrange("(r g) -> r g", r=ROWS), base_i[:]).then_inc(s_base_w, 16)
            sp.wait_ge(s_base_w, 16)
            sp.dma_start(base_row[:], base_dram.rearrange("(o t) -> o t", o=1)).then_inc(s_base_r, 16)
            for n, (c, m) in enumerate(CHUNKS):
                sp.wait_ge(s_hr, n + 1)
                sp.dma_start(node_view(h_dram)[:, c:c + m, :], h_rows[:, c:c + m, :]).then_inc(s_hd, 16)
            sp.wait_ge(s_hd, 16 * len(CHUNKS))
            sp.wait_ge(s_fin, 1)
            sp.dma_start(node_view(out), h_rows[:]).then_inc(s_out, 16)
            sp.wait_ge(s_out, 16)

        @block.gpsimd
        def _(pool):
            nc.gpsimd.memset(ident[:], 0.0).then_inc(s_zero, 1)
            pool.wait_ge(s_zero, 1)
            nc.gpsimd.affine_select(out=ident[:], in_=ident[:], compare_op=ALU.not_equal, fill=1.0, base=0,
                                    pattern=[[-1, 128]], channel_multiplier=1).then_inc(s_const, 1)
            nc.gpsimd.iota(iotaN[:], pattern=[[1, NPAD]], base=0, channel_multiplier=0,
                           allow_small_or_imprecise_dtypes=True).then_inc(s_const, 1)
            pool.wait_ge(s_flag, 1)
            general = pool.value_load(flag_i[0:1, 0:1], min_val=0, max_val=1)
            for l in range(2):
                table = (x, h_dram)[l]
                if l == 1:
                    for n, (c, m) in enumerate(CHUNKS):
                        pool.wait_ge(s_dense, n + 1)
                        nc.gpsimd.memset(acc[0:C, :, c * P:(c + m) * P], 0.0).then_inc(s_clear, 1)
                    pool.wait_ge(s_hd, 16 * len(CHUNKS))
                with pool.Fori(0, LOOPS) as i:
                    for h in range(2):
                        pool.wait_ge(s_idx[h], i + (l * LOOPS + 1))
                        pool.sem_inc(s_go, 1)
                        for u in range(U):
                            pool.indirect_dma_start(xg[:, h, u, :], None, table,
                                                    bass.IndirectOffsetOnAxis(idx[:, h, u:u + 1], 0),
                                                    ).then_inc(s_gather[h], 16)
                with pool.If(general):
                    with pool.Fori(0, T) as t:
                        pool.wait_ge(s_gi[l], t + 1)
                        pool.sem_inc(s_go, 1)
                        pool.indirect_dma_start(gen_x[:], None, table,
                                                bass.IndirectOffsetOnAxis(gen_idx[:, 0:1], 0),
                                                ).then_inc(s_gx[l], 16)

        def evacuate(eng, copy, n):
            kind, h = BATCHES[n]
            eng.wait_ge(s_tr, n + 1)
            if kind == "x":
                c, m = CHUNKS[h]
                i = copy(acc[C:2 * C, KH - 1, c * P:(c + m) * P], ps_t[n % 2][0:C, 0:m * P])
            else:
                to = {"src": srcT[:], "rel": relT[:], "far": farT[:], "v0": vT[:, 0], "v1": vT[:, 1]}[kind]
                tiles = to.rearrange("p (r g) -> p g r", g=RG)[:, h * HALF:(h + 1) * HALF, :]
                i = copy(tiles, ps_t[n % 2][0:P, 0:HALF * ROWS].rearrange("p (g r) -> p g r", g=HALF))
            i.then_inc(s_ev[n % 2], 1)

        @block.scalar
        def _(act):
            for n in range(NBATCH):
                evacuate(act, nc.scalar.copy, n)
            act.wait_ge(s_ev[0], (NBATCH + 1) // 2)
            act.wait_ge(s_flag, 1)
            general = act.value_load(flag_i[0:1, 0:1], min_val=0, max_val=1)
            act.wait_ge(s_w, 16 * 8)
            for l in range(2):
                with act.Fori(0, LOOPS) as i:
                    for h in range(2):
                        act.wait_ge(s_mm[h], i + (l * LOOPS + 1))
                        nc.scalar.copy(idx[:, h, :], srcT[:, bass.ds(i * (2 * U) + h * U, U)]).then_inc(s_idx[h], 1)
                with act.If(general):
                    with act.Fori(0, T) as t:
                        nc.scalar.copy(gen_idx[:], srcT[:, bass.ds(t, 1)]).then_inc(s_gi[l], 1)
                        act.wait_ge(s_gm[l], t * WINDOWS + WINDOWS)
                for n, (c, m) in enumerate(CHUNKS):
                    d = l * len(CHUNKS) + n
                    act.wait_ge(s_dense, d + 1)
                    if l == 0:
                        to = acc[C:2 * C, KH - 1, c * P:(c + m) * P]
                    else:
                        if n >= 2:
                            act.wait_ge(s_ht, d - 1)
                        to = outT[C:2 * C, n % 2, 0:m * P]
                    nc.scalar.activation(to, ps_d[n % 2][C:2 * C, 0:m * P], ACT.Relu,
                                         bias=bias[l][C:2 * C, :]).then_inc(s_relu, 1)
            act.wait_ge(s_var, 1)
            nc.scalar.activation(ystd[:], yvar[:], ACT.Sqrt, bias=eps[:], scale=1.0 / C).then_inc(s_std, 1)

        def turn_back(pe, l, n):
            c, m = CHUNKS[n]
            d = l * len(CHUNKS) + n
            pe.wait_ge(s_relu, d + 1)
            if d >= 2:
                pe.wait_ge(s_hr, d - 1)
            for j in range(m):
                cols = acc[C:2 * C, KH - 1, (c + j) * P:(c + j + 1) * P] if l == 0 \
                    else outT[C:2 * C, n % 2, j * P:(j + 1) * P]
                last = nc.tensor.transpose(ps_t[d % 2][0:P, j * C:(j + 1) * C], cols, ident[C:2 * C, C:2 * C])
            last.then_inc(s_ht, 1)

        @block.tensor
        def _(pe):
            for h in range(2):
                pe.sem_inc(s_mm[h], 1)
            pe.wait_ge(s_const, 1)
            for n, (kind, h) in enumerate(BATCHES):
                if n >= 2:
                    pe.wait_ge(s_ev[n % 2], n // 2)
                if kind == "src":
                    pe.wait_ge(s_rows, 1)
                elif kind == "rel":
                    pe.wait_ge(s_rows, 3)
                elif kind == "far":
                    pe.wait_ge(s_rows, 4)
                elif kind == "x":
                    pe.wait_ge(s_x, 16)
                else:
                    pe.wait_ge(s_attr, 16)
                if kind == "x":
                    c, m = CHUNKS[h]
                    for j in range(m):
                        last = nc.tensor.transpose(ps_t[n % 2][0:C, j * P:(j + 1) * P], x_rows[:, c + j, :],
                                                   ident[0:P, 0:P])
                else:
                    for j in range(HALF):
                        g = h * HALF + j
                        rows = {"src": src_f, "rel": rel_f, "far": dst_f}[kind][:, g, :] if kind[0] != "v" \
                            else attr_r[:, g, :, int(kind[1])]
                        last = nc.tensor.transpose(ps_t[n % 2][0:P, j * ROWS:(j + 1) * ROWS], rows,
                                                   ident[0:ROWS, 0:ROWS])
                last.then_inc(s_tr, 1)
            pe.wait_ge(s_far, 1)
            nc.tensor.transpose(ps_g[0:1, 0:ROWS], far_col[:], ident[0:ROWS, 0:ROWS]).then_inc(s_flagT, 1)
            pe.wait_ge(s_flag, 1)
            general = pe.value_load(flag_i[0:1, 0:1], min_val=0, max_val=1)
            pe.wait_ge(s_w, 16 * 8)
            for l in range(2):
                with pe.Fori(0, LOOPS) as i:
                    for h in range(2):
                        pe.wait_ge(s_rhs[h], i + (l * LOOPS + 1))
                        pe.wait_ge(s_gather[h], i * (16 * U) + (l * LOOPS + 1) * 16 * U)
                        for u in range(U):
                            for half in range(2):
                                last = nc.tensor.matmul(
                                    ps_e[h][half * C:(half + 1) * C, u * KH * W:(u + 1) * KH * W],
                                    xg[:, h, u, :], rhs[:, h, u, half * KH:(half + 1) * KH, :],
                                    start=True, stop=True)
                        last.then_inc(s_mm[h], 1)
                with pe.If(general):
                    with pe.Fori(0, T) as t:
                        with pe.Fori(0, WINDOWS) as w:
                            pe.wait_ge(s_gx[l], t * 16 + 16)
                            pe.wait_ge(s_gr[l], t * WINDOWS + w + 1)
                            for half in range(2):
                                last = nc.tensor.matmul(ps_g[half * C:(half + 1) * C, 0:KH * WG], gen_x[:],
                                                        gen_rhs[:, half * KH:(half + 1) * KH, :],
                                                        start=True, stop=True)
                            last.then_inc(s_gm[l], 1)
                pe.wait_ge(s_acc, l + 1)
                for n, (c, m) in enumerate(CHUNKS):
                    d = l * len(CHUNKS) + n
                    if d >= 2:
                        pe.wait_ge(s_relu, d - 1)
                    for k in range(KH):
                        last = nc.tensor.matmul(ps_d[n % 2][C:2 * C, 0:m * P], wst[l][:, k, :],
                                                acc[:, k, c * P:(c + m) * P], start=(k == 0), stop=(k == KH - 1))
                    last.then_inc(s_dense, 1)
                    if n:
                        turn_back(pe, l, n - 1)
                turn_back(pe, l, len(CHUNKS) - 1)

        @block.vector
        def _(dve):
            chain = [0]

            def link(ins):
                chain[0] += 1
                ins.then_inc(s_dve, 1)
                dve.wait_ge(s_dve, chain[0])

            nc.vector.memset(eps[:], EPS)
            dve.sem_inc(s_add, 1)
            nc.vector.memset(basis[:, :, K:2 * KH], 0.0)
            nc.vector.memset(acc[C:2 * C, KH - 1, NODES:NPAD], 0.0)
            nc.vector.memset(acc[0:C], 0.0)
            link(nc.vector.memset(acc[C:2 * C, 0:KH - 1], 0.0))
            dve.wait_ge(s_src, 16)
            nc.vector.tensor_copy(src_f[:], src_i[:]).then_inc(s_rows, 1)
            dve.wait_ge(s_dst, 16)
            link(nc.vector.tensor_copy(dst_f[:], dst_i[:]))
            link(nc.vector.tensor_reduce(base_f[:], dst_f[:], AX, ALU.min))
            nc.vector.tensor_copy(base_i[:], base_f[:]).then_inc(s_rows, 1)
            base_b = base_f[:].rearrange("r (g o) -> r g o", o=1).broadcast_to([ROWS, RG, P])
            nc.vector.tensor_tensor(rel_f[:], dst_f[:], base_b, ALU.subtract).then_inc(s_rows, 1)
            dve.wait_ge(s_rows, 3)
            nc.vector.tensor_reduce(far_col[:], rel_f[:].rearrange("r g p -> r (g p)"), AX, ALU.max).then_inc(s_far, 1)
            link(nc.vector.tensor_scalar(near_f[:], rel_f[:], float(W), FAR, ALU.is_lt, ALU.mult))
            nc.vector.tensor_tensor(dst_f[:], dst_f[:], near_f[:], ALU.add).then_inc(s_rows, 1)
            dve.wait_ge(s_flagT, 1)
            link(nc.vector.tensor_reduce(far_one[:], ps_g[0:1, 0:ROWS], AX, ALU.max))
            nc.vector.tensor_scalar(flag_i[:], far_one[:], float(W), None, ALU.is_ge).then_inc(s_flag, 1)
            dve.wait_ge(s_ev[0], BASIS_READY[0])
            dve.wait_ge(s_ev[1], BASIS_READY[1])
            link(nc.vector.scalar_tensor_tensor(quad[:, :, 2, :], vT[:], 0.5, vT[:], ALU.mult, ALU.mult))
            link(nc.vector.tensor_tensor(quad[:, :, 0, :], quad[:, :, 2, :], vT[:], ALU.subtract))
            link(nc.vector.scalar_tensor_tensor(quad[:, :, 1, :], quad[:, :, 0, :], 0.0, quad[:, :, 2, :],
                                                ALU.add, ALU.add))
            nc.vector.tensor_scalar(quad[:, :, 1, :], quad[:, :, 1, :], -1.0, 0.5, ALU.mult, ALU.add)
            link(nc.vector.tensor_scalar(quad[:, :, 0, :], quad[:, :, 0, :], 1.0, 0.5, ALU.mult, ALU.add))
            for i in range(3):
                k3 = basis[:, :, 3 * i:3 * i + 3].rearrange("p t k -> p k t")
                first = quad[:, 0, i:i + 1, :].broadcast_to([P, 3, T])
                last = nc.vector.tensor_tensor(k3, first, quad[:, 1, :, :], ALU.mult)
            link(last)
            dve.wait_ge(s_const, 2)
            dve.wait_ge(s_ev[0], (NBATCH + 1) // 2)
            dve.wait_ge(s_ev[1], NBATCH // 2)
            dve.wait_ge(s_base_r, 16)
            general = dve.value_load(flag_i[0:1, 0:1], min_val=0, max_val=1)
            for l in range(2):
                if l == 1:
                    dve.wait_ge(s_clear, 2 * len(CHUNKS))
                with dve.Fori(0, LOOPS) as i:
                    for h in range(2):
                        n0 = l * 2 * LOOPS + h
                        dve.wait_ge(s_mm[h], i + (l * LOOPS + 1))
                        rel = relT[:, bass.ds(i * (2 * U) + h * U, U)]
                        nc.vector.tensor_tensor(
                            hot[:, h], iotaN[:, 0:W].rearrange("p (o w) -> p o w", o=1).broadcast_to([P, U, W]),
                            rel.rearrange("p (u o) -> p u o", o=1).broadcast_to([P, U, W]), ALU.is_equal,
                        ).then_inc(s_hot, 1)
                        dve.wait_ge(s_hot, i * 2 + (n0 + 1))
                        b = basis[:, bass.ds(i * (2 * U) + h * U, U), :]
                        nc.vector.tensor_tensor(
                            rhs[:, h], b.rearrange("p u (k o) -> p u k o", o=1).broadcast_to([P, U, 2 * KH, W]),
                            hot[:, h].rearrange("p u (o w) -> p u o w", o=1).broadcast_to([P, U, 2 * KH, W]),
                            ALU.mult).then_inc(s_rhs[h], 1)
                    for h in range(2):
                        t0 = l * T + h * U
                        _, at = nc.values_load_multi_w_load_instructions(
                            base_row[0:1, bass.ds(i * (2 * U) + h * U, U)], engines=DVE_ONLY, min_val=0,
                            max_val=NODES - 1, skip_runtime_bounds_check_because="a destination is a node")
                        dve.wait_ge(s_mm[h], i + (l * LOOPS + 2))
                        for u in range(U):
                            dve.wait_ge(s_add, i * (2 * U) + (t0 + u + 1))
                            window = acc[:, :, bass.ds(at[u], W)]
                            part = ps_e[h][:, u * KH * W:(u + 1) * KH * W].rearrange("c (k w) -> c k w", w=W)
                            nc.vector.tensor_tensor(window, window, part, ALU.add).then_inc(s_add, 1)
                dve.wait_ge(s_add, (l + 1) * T + 1)
                with dve.If(general):
                    with dve.Fori(0, T) as t:
                        b = basis[:, bass.ds(t, 1), :].rearrange("p o k -> p (o k)")
                        with dve.Fori(0, WINDOWS) as w:
                            nc.vector.tensor_scalar(gen_hot[:], iotaN[:, bass.ds(w * WG, WG)],
                                                    farT[:, bass.ds(t, 1)], None, ALU.is_equal).then_inc(s_gh[l], 1)
                            dve.wait_ge(s_gh[l], t * WINDOWS + w + 1)
                            nc.vector.tensor_tensor(
                                gen_rhs[:], b.rearrange("p (k o) -> p k o", o=1).broadcast_to([P, 2 * KH, WG]),
                                gen_hot[:].rearrange("p (o w) -> p o w", o=1).broadcast_to([P, 2 * KH, WG]),
                                ALU.mult).then_inc(s_gr[l], 1)
                            dve.wait_ge(s_gm[l], t * WINDOWS + w + 1)
                            window = acc[:, :, bass.ds(w * WG, WG)]
                            nc.vector.tensor_tensor(
                                window, window, ps_g[:, 0:KH * WG].rearrange("c (k w) -> c k w", w=WG), ALU.add,
                            ).then_inc(s_ga[l], 1)
                            dve.wait_ge(s_ga[l], t * WINDOWS + w + 1)
                nc.vector.memset(mark[:], 0.0).then_inc(s_acc, 1)
                for n, (c, m) in enumerate(CHUNKS):
                    d = l * len(CHUNKS) + n
                    dve.wait_ge(s_ht, d + 1)
                    rows = ps_t[d % 2][0:P, 0:m * C].rearrange("p (j c) -> p j c", c=C)
                    y = h_rows[:, c:c + m, :]
                    if l == 0:
                        nc.vector.tensor_copy(y, rows).then_inc(s_hr, 1)
                        nc.vector.memset(acc[C:2 * C, 0:KH - 1, c * P:(c + m) * P], 0.0).then_inc(s_clear, 1)
                    else:
                        if n == 0:
                            dve.wait_ge(s_hd, 16 * len(CHUNKS))
                        nc.vector.tensor_tensor(y, rows, x_rows[:, c:c + m, :], ALU.add).then_inc(s_hr, 1)
                        dve.wait_ge(s_hr, d + 1)
                        spread = lambda a: a.rearrange("p (j o) -> p j o", o=1).broadcast_to([P, m, C])
                        link(nc.vector.tensor_reduce(ysum[:, c:c + m], y, AX, ALU.add))
                        link(nc.vector.tensor_scalar(ysum[:, c:c + m], ysum[:, c:c + m], -1.0 / C, None, ALU.mult))
                        link(nc.vector.tensor_tensor(y, y, spread(ysum[:, c:c + m]), ALU.add))
                        link(nc.vector.tensor_tensor(ysq[:, 0:m, :], y, y, ALU.mult))
                        link(nc.vector.tensor_reduce(yvar[:, c:c + m], ysq[:, 0:m, :], AX, ALU.add))
            nc.vector.memset(mark[:], 0.0).then_inc(s_var, 1)
            dve.wait_ge(s_std, 1)
            link(nc.vector.reciprocal(yrstd[:], ystd[:]))
            nc.vector.tensor_tensor(h_rows[:], h_rows[:],
                                    yrstd[:].rearrange("p (j o) -> p j o", o=1).broadcast_to([P, NB, C]),
                                    ALU.mult).then_inc(s_fin, 1)


_INS = ['x', 'src', 'dst', 'edge_attr_2', 'L0_gnn_W1', 'L0_gnn_root1', 'L0_gnn_b1', 'L0_gnn_W2', 'L0_gnn_root2',
        'L0_gnn_b2']


def kernel(**inputs):
    import numpy as _np
    import concourse.bacc as _bacc
    from concourse import mybir as _mybir
    from concourse.bass_utils import run_bass_kernel_spmd as _run

    nc = _bacc.Bacc("TRN2", target_bir_lowering=False, num_devices=1)
    arrays, args = {}, []
    for name in _INS:
        a = _np.ascontiguousarray(inputs[name])
        arrays[f"in_{name}_dram"] = a
        args.append(nc.dram_tensor(f"in_{name}_dram", a.shape, _mybir.dt.from_np(a.dtype), kind="ExternalInput").ap())
    out = nc.dram_tensor("out_0_dram", (3125, 64), _mybir.dt.float32, kind="ExternalOutput").ap()
    spline_gnn_program(nc, *args, out)
    r = _run(nc, [arrays], core_ids=[0])
    return r.results[0]["out_0_dram"]
```

```python
import concourse.bass as bass
from concourse import mybir
from contextlib import ExitStack


def spline_gnn_program(nc, x, src, dst, attr, W1, root1, b1, W2, root2, b2, out):
    fp32 = mybir.dt.float32
    i32 = mybir.dt.int32
    i16 = mybir.dt.int16
    fp16 = mybir.dt.float16
    bf16 = mybir.dt.bfloat16
    ALU = mybir.AluOpType
    ACT = mybir.ActivationFunctionType
    AX = mybir.AxisListType.X
    DVE_ONLY = [mybir.EngineType.DVE]

    NODES, C = x.shape
    EDGES = src.shape[0]
    K = W1.shape[0]
    KH = (K + 1) // 2
    EPS = 1e-5

    P = 125
    T = EDGES // P
    U = 4
    G = 4
    D = G - 1
    BT = U * G
    BODIES = T // BT
    PAIRS = BODIES // 2
    NB = NODES // P
    FIFTHS, NQ = 5, NB // 5
    ROWS = 100
    RG = T // ROWS
    W = 8
    WG = 100
    WINDOWS = -(-NODES // WG)
    NPAD = WINDOWS * WG
    FAR = 65536.0
    MID = NODES // 2
    PW = U * P + 4
    CB = 4
    CHUNKS = [(c, min(CB, NB - c)) for c in range(0, NB, CB)]
    LAYERS = [(W1, root1, b1), (W2, root2, b2)]
    assert NODES - MID + P <= 2048 and T * P == EDGES and NB * P == NODES and PAIRS * 2 * BT == T and NB % FIFTHS == 0 and RG * ROWS == T

    ctx = ExitStack()
    with ctx:
        def sb(name, shape, dt=fp32):
            return ctx.enter_context(nc.sbuf_tensor(name, shape, dt))

        def pb(name, shape):
            return ctx.enter_context(nc.psum_tensor(name, shape, fp32))

        def sem(name):
            return ctx.enter_context(nc.semaphore(name))

        h_dram = nc.dram_tensor("h_dram", (NODES, C), fp32, kind="Internal").ap()
        src16_dram = nc.dram_tensor("src16_dram", (EDGES,), fp16, kind="Internal").ap()
        base_dram = nc.dram_tensor("base_dram", (T,), i32, kind="Internal").ap()

        stage = sb("stage", [128, 8 * RG * P])
        row_table = lambda n, m=1: stage[0:ROWS, n * RG * P:(n + m) * RG * P]
        by_tile = lambda a: a.rearrange("r (g p) -> r g p", p=P)
        src_i = by_tile(row_table(0).bitcast(i32))
        dst_i = by_tile(row_table(1).bitcast(i32))
        src_f = by_tile(row_table(2))
        dst_f = by_tile(row_table(3))
        rel_f = by_tile(row_table(4))
        near_f = by_tile(row_table(5))
        attr_r = row_table(6, 2).rearrange("r (g p v) -> r g p v", p=P, v=2)
        mark = sb("mark", [1, 1])
        src_16 = sb("src_16", [ROWS, RG, P], fp16)
        base_f = sb("base_f", [ROWS, RG])
        base_i = sb("base_i", [ROWS, RG], i32)
        far_col = sb("far_col", [ROWS, 1])
        far_one = sb("far_one", [1, 1])
        flag_i = sb("flag_i", [1, 1], i32)
        base_row = sb("base_row", [1, T], i32)
        srcT = sb("srcT", [P, T])
        relT = sb("relT", [P, T + BT])
        farT = sb("farT", [P, T])
        vT = sb("vT", [P, 2, T])
        quad = stage[0:P, 0:2 * 3 * T].rearrange("p (v n t) -> p v n t", v=2, n=3)
        basis = sb("basis", [P, T + BT, 2 * KH])
        ident = sb("ident", [128, 128])
        iotaN = sb("iotaN", [P, NPAD], i16)
        wst = [sb(f"wst{l}", [128, KH, C]) for l in range(2)]
        bias = [sb(f"bias{l}", [128, 1]) for l in range(2)]
        x_rows = sb("x_rows", [P, NB, C])
        h_rows = sb("h_rows", [P, NB, C])
        acc = sb("acc", [128, KH, NPAD])
        outT = sb("outT", [128, 2, CB * P])
        idx = sb("idx", [P, 2, D, U], i32)
        xg = sb("xg", [P, G, U, C])
        hot = sb("hot", [P, G, U, W])
        rhs = sb("rhs", [P, G, U, 2 * KH, W])
        src_b = sb("src_b", [P, 2, U * P], fp16)
        src_p = sb("src_p", [P, PW], fp16)
        lane = sb("lane", [P, 1])
        pick = stage[0:P, 0:NB * PW // 2].bitcast(bf16).rearrange("p (j e) -> p j e", e=PW)
        parts = sb("parts", [P, NB, 3, C], bf16)
        rest = sb("rest", [P, CB, C])
        gen_idx = sb("gen_idx", [P, 1], i32)
        gen_x = sb("gen_x", [P, C])
        gen_hot = sb("gen_hot", [P, WG])
        gen_rhs = sb("gen_rhs", [P, 2 * KH, WG])
        ysum = sb("ysum", [P, NB])
        ysq = sb("ysq", [P, CB, C])
        yvar = sb("yvar", [P, NB])
        ystd = sb("ystd", [P, NB])
        yrstd = sb("yrstd", [P, NB])
        eps = sb("eps", [P, 1])

        ps_p = pb("ps_p", [128, U, 512])
        ps_t = [ps_p[:, i] for i in range(2)]
        ps_d = [ps_p[:, i + 2] for i in range(2)]
        ps_e = [pb(f"ps_e{i}", [128, 512]) for i in range(G)]
        ps_g = ps_e[D]

        s_src = sem("s_src")
        s_dst = sem("s_dst")
        s_attr = sem("s_attr")
        s_x = sem("s_x")
        s_w = sem("s_w")
        s_const = sem("s_const")
        s_zero = sem("s_zero")
        s_rows = sem("s_rows")
        s_dve = sem("s_dve")
        s_tr = sem("s_tr")
        s_ev = [sem(f"s_ev{i}") for i in range(2)]
        s_base_w = sem("s_base_w")
        s_base_r = sem("s_base_r")
        s_far = sem("s_far")
        s_flagT = sem("s_flagT")
        s_flag = sem("s_flag")
        s_vT = sem("s_vT")
        s_basis = sem("s_basis")
        s_idx = [sem(f"s_idx{i}") for i in range(2)]
        s_gather = [sem(f"s_gather{i}") for i in range(D)]
        s_src16 = sem("s_src16")
        s_src_b = [sem(f"s_src_b{i}") for i in range(2)]
        s_pick = sem("s_pick")
        s_used = sem("s_used")
        s_kept = sem("s_kept")
        s_picked = sem("s_picked")
        s_lane = sem("s_lane")
        s_mid = sem("s_mid")
        s_parts = sem("s_parts")
        s_go = sem("s_go")
        s_hot = sem("s_hot")
        s_rhs = [sem(f"s_rhs{i}") for i in range(G)]
        s_mm = [sem(f"s_mm{i}") for i in range(G)]
        s_add = sem("s_add")
        s_acc = sem("s_acc")
        s_gi = [sem(f"s_gi{i}") for i in range(2)]
        s_gx = [sem(f"s_gx{i}") for i in range(2)]
        s_gh = [sem(f"s_gh{i}") for i in range(2)]
        s_gr = [sem(f"s_gr{i}") for i in range(2)]
        s_gm = [sem(f"s_gm{i}") for i in range(2)]
        s_ga = [sem(f"s_ga{i}") for i in range(2)]
        s_dense = sem("s_dense")
        s_relu = sem("s_relu")
        s_ht = sem("s_ht")
        s_hr = sem("s_hr")
        s_hd = sem("s_hd")
        s_clear = sem("s_clear")
        s_var = sem("s_var")
        s_std = sem("s_std")
        s_fin = sem("s_fin")
        s_out = sem("s_out")

        block = ctx.enter_context(nc.Block())

        rows_view = lambda a: a.rearrange("(r g p) -> r g p", r=ROWS, p=P)
        node_view = lambda a: a.rearrange("(j p) c -> p j c", p=P)
        HALF = RG // 2
        BATCHES = [(n, h) for n in ("src", "rel", "far", "v0", "v1") for h in range(2)] + \
                  [("x", c) for c in range(len(CHUNKS))]
        NBATCH = len(BATCHES)
        TABLES = 5 * 2

        @block.sync
        def _(sp):
            sp.dma_start(src_i, rows_view(src)).then_inc(s_src, 16)
            sp.dma_start(dst_i, rows_view(dst)).then_inc(s_dst, 16)
            sp.dma_start(attr_r, attr.rearrange("(r g p) v -> r g p v", r=ROWS, p=P)).then_inc(s_attr, 16)
            sp.dma_start(x_rows[:], node_view(x)).then_inc(s_x, 16)
            for l, (Wl, root, b) in enumerate(LAYERS):
                sp.dma_start(wst[l][0:C], Wl[0:KH].rearrange("k c o -> c k o")).then_inc(s_w, 16)
                sp.dma_start(wst[l][C:2 * C, 0:K - KH], Wl[KH:K].rearrange("k c o -> c k o")).then_inc(s_w, 16)
                sp.dma_start(wst[l][C:2 * C, K - KH], root).then_inc(s_w, 16)
                sp.dma_start(bias[l][C:2 * C, :], b.rearrange("(c o) -> c o", o=1)).then_inc(s_w, 16)
            sp.wait_ge(s_rows, 2)
            sp.dma_start(base_dram.rearrange("(r g) -> r g", r=ROWS), base_i[:]).then_inc(s_base_w, 16)
            sp.wait_ge(s_base_w, 16)
            sp.dma_start(base_row[:], base_dram.rearrange("(o t) -> o t", o=1)).then_inc(s_base_r, 16)
            sp.wait_ge(s_rows, 5)
            sp.dma_start(src16_dram.rearrange("(r g p) -> r g p", r=ROWS, p=P), src_16[:]).then_inc(s_src16, 16)
            sp.wait_ge(s_src16, 16)

            def load_sources(slot, body):
                edges = src16_dram.rearrange("(o e) -> o e", o=1)[:, bass.ds(body * (BT * P) + D * U * P, U * P)]
                sp.dma_start(src_b[:, slot, :], edges.broadcast_to([P, U * P])).then_inc(s_src_b[slot], 16)

            def load_loop(l):
                with sp.Fori(0, PAIRS - 1) as j:
                    for b in range(2):
                        sp.wait_ge(s_pick, j * (2 * FIFTHS) + FIFTHS * (l * BODIES + b + 1))
                        load_sources(b, j * 2 + (b + 2))

            for b in range(2):
                load_sources(b, b)
            load_loop(0)
            for b in range(2):
                sp.wait_ge(s_pick, FIFTHS * (BODIES + b - 1))
                load_sources(b, b)
            for n, (c, m) in enumerate(CHUNKS):
                sp.wait_ge(s_hr, n + 1)
                sp.dma_start(node_view(h_dram)[:, c:c + m, :], h_rows[:, c:c + m, :]).then_inc(s_hd, 16)
            sp.wait_ge(s_hd, 16 * len(CHUNKS))
            load_loop(1)
            sp.wait_ge(s_pick, FIFTHS * (2 * BODIES - 1))
            load_sources(0, 0)
            sp.wait_ge(s_src_b[0], 16 * (BODIES + 1))
            sp.wait_ge(s_fin, 1)
            sp.dma_start(node_view(out), h_rows[:]).then_inc(s_out, 16)
            sp.wait_ge(s_out, 16)

        @block.gpsimd
        def _(pool):
            nc.gpsimd.memset(ident[:], 0.0).then_inc(s_zero, 1)
            pool.wait_ge(s_zero, 1)
            nc.gpsimd.affine_select(out=ident[:], in_=ident[:], compare_op=ALU.not_equal, fill=1.0, base=0,
                                    pattern=[[-1, 128]], channel_multiplier=1).then_inc(s_const, 1)
            nc.gpsimd.iota(iotaN[:], pattern=[[1, NPAD]], base=0, channel_multiplier=0,
                           allow_small_or_imprecise_dtypes=True).then_inc(s_const, 1)
            nc.gpsimd.iota(lane[:], pattern=[[0, 1]], base=0, channel_multiplier=1,
                           allow_small_or_imprecise_dtypes=True).then_inc(s_const, 1)
            pool.wait_ge(s_flag, 1)
            general = pool.value_load(flag_i[0:1, 0:1], min_val=0, max_val=1)
            for l in range(2):
                table = (x, h_dram)[l]
                if l == 1:
                    for n, (c, m) in enumerate(CHUNKS):
                        pool.wait_ge(s_dense, n + 1)
                        nc.gpsimd.memset(acc[0:C, :, c * P:(c + m) * P], 0.0).then_inc(s_clear, 1)
                    pool.wait_ge(s_hd, 16 * len(CHUNKS))
                with pool.Fori(0, PAIRS) as j:
                    for b in range(2):
                        for g in range(D):
                            if g == 0:
                                pool.wait_ge(s_idx[b], j + (l * PAIRS + 1))
                            pool.wait_ge(s_mm[g], j * 2 + (l * BODIES + b + 1))
                            pool.sem_inc(s_go, 1)
                            for u in range(U):
                                pool.indirect_dma_start(xg[:, g, u, :], None, table,
                                                        bass.IndirectOffsetOnAxis(idx[:, b, g, u:u + 1], 0),
                                                        ).then_inc(s_gather[g], 16)
                with pool.If(general):
                    with pool.Fori(0, T) as t:
                        pool.wait_ge(s_gi[l], t + 1)
                        pool.sem_inc(s_go, 1)
                        pool.indirect_dma_start(gen_x[:], None, table,
                                                bass.IndirectOffsetOnAxis(gen_idx[:, 0:1], 0),
                                                ).then_inc(s_gx[l], 16)

        def evacuate(eng, copy, n):
            kind, h = BATCHES[n]
            eng.wait_ge(s_tr, n + 1)
            if kind == "x":
                c, m = CHUNKS[h]
                i = copy(acc[C:2 * C, KH - 1, c * P:(c + m) * P], ps_t[n % 2][0:C, 0:m * P])
            else:
                to = {"src": srcT[:], "rel": relT[:, 0:T], "far": farT[:], "v0": vT[:, 0], "v1": vT[:, 1]}[kind]
                tiles = to.rearrange("p (r g) -> p g r", g=RG)[:, h * HALF:(h + 1) * HALF, :]
                i = copy(tiles, ps_t[n % 2][0:P, 0:HALF * ROWS].rearrange("p (g r) -> p g r", g=HALF))
            i.then_inc(s_ev[n % 2], 1)

        @block.scalar
        def _(act):
            for n in range(NBATCH):
                evacuate(act, nc.scalar.copy, n)
            act.wait_ge(s_ev[0], (NBATCH + 1) // 2)
            act.wait_ge(s_flag, 1)
            general = act.value_load(flag_i[0:1, 0:1], min_val=0, max_val=1)
            act.wait_ge(s_w, 16 * 8)

            def place_indices(slot, body):
                tiles = srcT[:, bass.ds(body * BT, D * U)].rearrange("p (g u) -> p g u", u=U)
                nc.scalar.copy(idx[:, slot], tiles).then_inc(s_idx[slot], 1)

            def keep_picked(body):
                act.wait_ge(s_used, body * FIFTHS + FIFTHS)
                act.wait_ge(s_mm[D], body + 1)
                nc.scalar.copy(xg[:, D], ps_p[0:P, :, 0:C]).then_inc(s_kept, 1)

            for b in range(2):
                place_indices(b, b)
            for l in range(2):
                with act.Fori(0, PAIRS - 1) as j:
                    for b in range(2):
                        keep_picked(j * 2 + (l * BODIES + b))
                        act.wait_ge(s_mm[D - 1], j * 2 + (l * BODIES + b + 2))
                        place_indices(b, j * 2 + (b + 2))
                for b in range(2):
                    keep_picked((l + 1) * BODIES - 2 + b)
                    if l == 0:
                        act.wait_ge(s_mm[D - 1], BODIES + b)
                        place_indices(b, b)
                with act.If(general):
                    with act.Fori(0, T) as t:
                        nc.scalar.copy(gen_idx[:], srcT[:, bass.ds(t, 1)]).then_inc(s_gi[l], 1)
                        act.wait_ge(s_gm[l], t * WINDOWS + WINDOWS)
                for n, (c, m) in enumerate(CHUNKS):
                    d = l * len(CHUNKS) + n
                    act.wait_ge(s_dense, d + 1)
                    if l == 0:
                        to = acc[C:2 * C, KH - 1, c * P:(c + m) * P]
                    else:
                        if n >= 2:
                            act.wait_ge(s_ht, d - 1)
                        to = outT[C:2 * C, n % 2, 0:m * P]
                    nc.scalar.activation(to, ps_d[n % 2][C:2 * C, 0:m * P], ACT.Relu,
                                         bias=bias[l][C:2 * C, :]).then_inc(s_relu, 1)
            act.wait_ge(s_var, 1)
            nc.scalar.activation(ystd[:], yvar[:], ACT.Sqrt, bias=eps[:], scale=1.0 / C).then_inc(s_std, 1)

        def turn_back(pe, l, n):
            c, m = CHUNKS[n]
            d = l * len(CHUNKS) + n
            pe.wait_ge(s_relu, d + 1)
            if d >= 2:
                pe.wait_ge(s_hr, d - 1)
            for j in range(m):
                cols = acc[C:2 * C, KH - 1, (c + j) * P:(c + j + 1) * P] if l == 0 \
                    else outT[C:2 * C, n % 2, j * P:(j + 1) * P]
                last = nc.tensor.transpose(ps_t[d % 2][0:P, j * C:(j + 1) * C], cols, ident[C:2 * C, C:2 * C])
            last.then_inc(s_ht, 1)

        @block.tensor
        def _(pe):
            for g in range(G):
                pe.sem_inc(s_mm[g], 1)
            pe.sem_inc(s_picked, 1)
            pe.wait_ge(s_const, 1)
            for n, (kind, h) in enumerate(BATCHES):
                if n >= 2:
                    pe.wait_ge(s_ev[n % 2], n // 2)
                if kind == "src":
                    pe.wait_ge(s_rows, 1)
                elif kind == "rel":
                    pe.wait_ge(s_rows, 3)
                elif kind == "far":
                    pe.wait_ge(s_rows, 4)
                elif kind == "x":
                    pe.wait_ge(s_x, 16)
                else:
                    pe.wait_ge(s_attr, 16)
                if kind == "x":
                    c, m = CHUNKS[h]
                    for j in range(m):
                        last = nc.tensor.transpose(ps_t[n % 2][0:C, j * P:(j + 1) * P], x_rows[:, c + j, :],
                                                   ident[0:P, 0:P])
                else:
                    for j in range(HALF):
                        g = h * HALF + j
                        rows = {"src": src_f, "rel": rel_f, "far": dst_f}[kind][:, g, :] if kind[0] != "v" \
                            else attr_r[:, g, :, int(kind[1])]
                        last = nc.tensor.transpose(ps_t[n % 2][0:P, j * ROWS:(j + 1) * ROWS], rows,
                                                   ident[0:ROWS, 0:ROWS])
                last.then_inc(s_tr, 1)
            pe.wait_ge(s_far, 1)
            nc.tensor.transpose(ps_g[0:1, 0:ROWS], far_col[:], ident[0:ROWS, 0:ROWS]).then_inc(s_flagT, 1)
            pe.wait_ge(s_flag, 1)
            general = pe.value_load(flag_i[0:1, 0:1], min_val=0, max_val=1)
            pe.wait_ge(s_w, 16 * 8)
            for l in range(2):
                if l == 1:
                    pe.wait_ge(s_hr, len(CHUNKS))
                    pe.wait_ge(s_relu, len(CHUNKS))
                pe.wait_ge(s_parts, (l + 1) * len(CHUNKS))
                with pe.Fori(0, BODIES) as i:
                    def pick_fifth(q):
                        pe.wait_ge(s_pick, i * FIFTHS + (l * BODIES * FIFTHS + q + 1))
                        if q == 0:
                            pe.wait_ge(s_picked, i + (l * BODIES + 1))
                        for j in range(q * NQ, (q + 1) * NQ):
                            for u in range(U):
                                last = nc.tensor.matmul(
                                    ps_p[:, u, 0:3 * C], pick[:, j, u * P:u * P + 128],
                                    parts[:, j].rearrange("p n c -> p (n c)"), start=(j == 0), stop=(j == NB - 1))
                        last.then_inc(s_used, 1)

                    def multiply(g):
                        pe.wait_ge(s_rhs[g], i + (l * BODIES + 1))
                        if g < D:
                            pe.wait_ge(s_gather[g], i * (16 * U) + (l * BODIES + 1) * 16 * U)
                        else:
                            pe.wait_ge(s_picked, i + (l * BODIES + 2))
                        for u in range(U):
                            for half in range(2):
                                last = nc.tensor.matmul(
                                    ps_e[g][half * C:(half + 1) * C, u * KH * W:(u + 1) * KH * W],
                                    xg[:, g, u, :], rhs[:, g, u, half * KH:(half + 1) * KH, :],
                                    start=True, stop=True)
                        last.then_inc(s_mm[g], 1)

                    pick_fifth(0)
                    multiply(0)
                    for q in range(1, FIFTHS):
                        pick_fifth(q)
                    for g in range(1, G):
                        multiply(g)
                with pe.If(general):
                    with pe.Fori(0, T) as t:
                        with pe.Fori(0, WINDOWS) as w:
                            pe.wait_ge(s_gx[l], t * 16 + 16)
                            pe.wait_ge(s_gr[l], t * WINDOWS + w + 1)
                            for half in range(2):
                                last = nc.tensor.matmul(ps_g[half * C:(half + 1) * C, 0:KH * WG], gen_x[:],
                                                        gen_rhs[:, half * KH:(half + 1) * KH, :],
                                                        start=True, stop=True)
                            last.then_inc(s_gm[l], 1)
                pe.wait_ge(s_acc, l + 1)
                for n, (c, m) in enumerate(CHUNKS):
                    d = l * len(CHUNKS) + n
                    if d >= 2:
                        pe.wait_ge(s_relu, d - 1)
                    for k in range(KH):
                        last = nc.tensor.matmul(ps_d[n % 2][C:2 * C, 0:m * P], wst[l][:, k, :],
                                                acc[:, k, c * P:(c + m) * P], start=(k == 0), stop=(k == KH - 1))
                    last.then_inc(s_dense, 1)
                    if n:
                        turn_back(pe, l, n - 1)
                turn_back(pe, l, len(CHUNKS) - 1)

        @block.vector
        def _(dve):
            chain = [0]

            def link(ins):
                chain[0] += 1
                ins.then_inc(s_dve, 1)
                dve.wait_ge(s_dve, chain[0])

            nc.vector.memset(eps[:], EPS)
            dve.sem_inc(s_add, 1)
            nc.vector.memset(basis[:, :, K:2 * KH], 0.0)
            nc.vector.memset(acc[C:2 * C, KH - 1, NODES:NPAD], 0.0)
            nc.vector.memset(acc[0:C], 0.0)
            link(nc.vector.memset(acc[C:2 * C, 0:KH - 1], 0.0))
            dve.wait_ge(s_src, 16)
            nc.vector.tensor_copy(src_f, src_i).then_inc(s_rows, 1)
            dve.wait_ge(s_dst, 16)
            link(nc.vector.tensor_copy(dst_f, dst_i))
            link(nc.vector.tensor_reduce(base_f[:], dst_f, AX, ALU.min))
            nc.vector.tensor_copy(base_i[:], base_f[:]).then_inc(s_rows, 1)
            base_b = base_f[:].rearrange("r (g o) -> r g o", o=1).broadcast_to([ROWS, RG, P])
            nc.vector.tensor_tensor(rel_f, dst_f, base_b, ALU.subtract).then_inc(s_rows, 1)
            dve.wait_ge(s_rows, 3)
            nc.vector.tensor_reduce(far_col[:], rel_f.rearrange("r g p -> r (g p)"), AX, ALU.max).then_inc(s_far, 1)
            link(nc.vector.tensor_scalar(near_f, rel_f, float(W), FAR, ALU.is_lt, ALU.mult))
            nc.vector.tensor_tensor(dst_f, dst_f, near_f, ALU.add).then_inc(s_rows, 1)
            nc.vector.tensor_scalar(src_16[:], src_i, float(MID), None, ALU.subtract).then_inc(s_rows, 1)
            dve.wait_ge(s_flagT, 1)
            link(nc.vector.tensor_reduce(far_one[:], ps_g[0:1, 0:ROWS], AX, ALU.max))
            nc.vector.tensor_scalar(flag_i[:], far_one[:], float(W), None, ALU.is_ge).then_inc(s_flag, 1)
            for b in range(2):
                dve.wait_ge(s_ev[b], TABLES // 2)
            link(nc.vector.scalar_tensor_tensor(quad[:, :, 2, :], vT[:], 0.5, vT[:], ALU.mult, ALU.mult))
            link(nc.vector.tensor_tensor(quad[:, :, 0, :], quad[:, :, 2, :], vT[:], ALU.subtract))
            link(nc.vector.scalar_tensor_tensor(quad[:, :, 1, :], quad[:, :, 0, :], 0.0, quad[:, :, 2, :],
                                                ALU.add, ALU.add))
            nc.vector.tensor_scalar(quad[:, :, 1, :], quad[:, :, 1, :], -1.0, 0.5, ALU.mult, ALU.add)
            link(nc.vector.tensor_scalar(quad[:, :, 0, :], quad[:, :, 0, :], 1.0, 0.5, ALU.mult, ALU.add))
            for i in range(3):
                k3 = basis[:, 0:T, 3 * i:3 * i + 3].rearrange("p t k -> p k t")
                first = quad[:, 0, i:i + 1, :].broadcast_to([P, 3, T])
                last = nc.vector.tensor_tensor(k3, first, quad[:, 1, :, :], ALU.mult)
            link(last)
            nc.vector.tensor_copy(basis[:, T:T + BT, :], basis[:, 0:BT, :])
            link(nc.vector.tensor_copy(relT[:, T:T + BT], relT[:, 0:BT]))
            dve.wait_ge(s_const, 2)
            dve.wait_ge(s_ev[0], (NBATCH + 1) // 2)
            dve.wait_ge(s_ev[1], NBATCH // 2)
            dve.wait_ge(s_base_r, 16)
            general = dve.value_load(flag_i[0:1, 0:1], min_val=0, max_val=1)
            def split(rows, c, m):
                hi, mid, lo = (parts[:, c:c + m, n, :] for n in range(3))
                link(nc.vector.tensor_copy(hi, rows))
                link(nc.vector.tensor_tensor(rest[:, 0:m, :], rows, hi, ALU.subtract))
                link(nc.vector.tensor_copy(mid, rest[:, 0:m, :]))
                nc.vector.tensor_tensor(lo, rest[:, 0:m, :], mid, ALU.subtract).then_inc(s_parts, 1)
                link(nc.vector.memset(mark[:], 0.0))

            def sources_by_lane(slot):
                nc.vector.tensor_scalar(src_p[:, 0:U * P], src_b[:, slot, :], lane[:], None,
                                        ALU.subtract).then_inc(s_lane, 1)

            def pick_block(j):
                return nc.vector.tensor_scalar(pick[:, j, :], src_p[:], float(P * j - MID), None, ALU.is_equal)

            def make_hot(tile):
                rel = relT[:, bass.ds(tile, BT)].rearrange("p (g u o) -> p g u o", g=G, o=1)
                window = iotaN[:, 0:W].rearrange("p (g u w) -> p g u w", g=1, u=1)
                nc.vector.tensor_tensor(hot[:], window.broadcast_to([P, G, U, W]), rel.broadcast_to([P, G, U, W]),
                                        ALU.is_equal).then_inc(s_hot, 1)

            def make_rhs(g, tile):
                bs = basis[:, bass.ds(tile, U), :]
                nc.vector.tensor_tensor(
                    rhs[:, g], bs.rearrange("p u (k o) -> p u k o", o=1).broadcast_to([P, U, 2 * KH, W]),
                    hot[:, g].rearrange("p u (o w) -> p u o w", o=1).broadcast_to([P, U, 2 * KH, W]),
                    ALU.mult).then_inc(s_rhs[g], 1)

            dve.wait_ge(s_x, 16)
            for c, m in CHUNKS:
                split(x_rows[:, c:c + m, :], c, m)
            dve.wait_ge(s_const, 3)
            link(nc.vector.memset(src_p[:, U * P:PW], FAR / 4))
            make_hot(0)
            dve.wait_ge(s_hot, 1)
            for g in range(G):
                make_rhs(g, g * U)
            dve.wait_ge(s_src_b[0], 16)
            sources_by_lane(0)
            dve.wait_ge(s_lane, 1)
            for q in range(FIFTHS):
                for j in range(q * NQ, (q + 1) * NQ):
                    last = pick_block(j)
                last.then_inc(s_pick, 1)
            for l in range(2):
                if l == 1:
                    dve.wait_ge(s_clear, 2 * len(CHUNKS))
                with dve.Fori(0, PAIRS) as i:
                    for b in range(2):
                        body = l * BODIES + b
                        first = lambda g: i * (2 * BT) + (b * BT + g * U)

                        def lowest(g):
                            _, at = nc.values_load_multi_w_load_instructions(
                                base_row[0:1, bass.ds(first(g), U)], engines=DVE_ONLY, min_val=0,
                                max_val=NODES - 1, skip_runtime_bounds_check_because="a destination is a node")
                            return at

                        def add_tile(g, u, at):
                            dve.wait_ge(s_add, i * (2 * BT) + (body * BT + g * U + u + 1))
                            window = acc[:, :, bass.ds(at[u], W)]
                            part = ps_e[g][:, u * KH * W:(u + 1) * KH * W].rearrange("c (k w) -> c k w", w=W)
                            nc.vector.tensor_tensor(window, window, part, ALU.add).then_inc(s_add, 1)

                        def multiplied(g):
                            dve.wait_ge(s_mm[g], i * 2 + (body + 2))

                        def fifth_used(q):
                            dve.wait_ge(s_used, i * (2 * FIFTHS) + (body * FIFTHS + q + 1))

                        at0 = lowest(0)
                        fifth_used(0)
                        dve.wait_ge(s_src_b[1 - b], i * 16 + 16 * (l * PAIRS + b + 1))
                        dve.wait_ge(s_pick, i * (2 * FIFTHS) + (body + 1) * FIFTHS)
                        sources_by_lane(1 - b)
                        multiplied(0)
                        dve.wait_ge(s_lane, i * 2 + (body + 2))
                        for u in range(U):
                            add_tile(0, u, at0)
                            pick_block(u)
                        pick_block(U).then_inc(s_pick, 1)
                        dve.wait_ge(s_rhs[D], i * 2 + (body + 1))
                        make_hot(first(0) + BT)
                        fifth_used(1)
                        for j in range(NQ, 2 * NQ):
                            last = pick_block(j)
                        last.then_inc(s_pick, 1)
                        dve.wait_ge(s_hot, i * 2 + (body + 2))
                        make_rhs(0, first(0) + BT)
                        at = [None] + [lowest(g) for g in range(1, G)]
                        rows = xg[:, D]
                        dve.wait_ge(s_kept, i * 2 + (body + 1))
                        nc.vector.tensor_tensor(rows, rows, ps_p[0:P, :, C:2 * C], ALU.add).then_inc(s_mid, 1)
                        pick_block(2 * NQ)
                        dve.wait_ge(s_mid, i * 2 + (body + 1))
                        nc.vector.tensor_tensor(rows, rows, ps_p[0:P, :, 2 * C:3 * C], ALU.add).then_inc(s_picked, 1)
                        for g in range(1, G):
                            blocks = range((g + 1) * NQ + (g == 1), (g + 2) * NQ)
                            fifth_used(g + 1)
                            multiplied(g)
                            for u in range(U):
                                add_tile(g, u, at[g])
                                last = pick_block(blocks[u])
                            if g > 1:
                                last = pick_block(blocks[U])
                            last.then_inc(s_pick, 1)
                            make_rhs(g, first(g) + BT)
                dve.wait_ge(s_add, (l + 1) * T + 1)
                with dve.If(general):
                    with dve.Fori(0, T) as t:
                        b = basis[:, bass.ds(t, 1), :].rearrange("p o k -> p (o k)")
                        with dve.Fori(0, WINDOWS) as w:
                            nc.vector.tensor_scalar(gen_hot[:], iotaN[:, bass.ds(w * WG, WG)],
                                                    farT[:, bass.ds(t, 1)], None, ALU.is_equal).then_inc(s_gh[l], 1)
                            dve.wait_ge(s_gh[l], t * WINDOWS + w + 1)
                            nc.vector.tensor_tensor(
                                gen_rhs[:], b.rearrange("p (k o) -> p k o", o=1).broadcast_to([P, 2 * KH, WG]),
                                gen_hot[:].rearrange("p (o w) -> p o w", o=1).broadcast_to([P, 2 * KH, WG]),
                                ALU.mult).then_inc(s_gr[l], 1)
                            dve.wait_ge(s_gm[l], t * WINDOWS + w + 1)
                            window = acc[:, :, bass.ds(w * WG, WG)]
                            nc.vector.tensor_tensor(
                                window, window, ps_g[:, 0:KH * WG].rearrange("c (k w) -> c k w", w=WG), ALU.add,
                            ).then_inc(s_ga[l], 1)
                            dve.wait_ge(s_ga[l], t * WINDOWS + w + 1)
                nc.vector.memset(mark[:], 0.0).then_inc(s_acc, 1)
                for n, (c, m) in enumerate(CHUNKS):
                    d = l * len(CHUNKS) + n
                    dve.wait_ge(s_ht, d + 1)
                    rows = ps_t[d % 2][0:P, 0:m * C].rearrange("p (j c) -> p j c", c=C)
                    y = h_rows[:, c:c + m, :]
                    if l == 0:
                        nc.vector.tensor_copy(y, rows).then_inc(s_hr, 1)
                        dve.wait_ge(s_hr, d + 1)
                        split(y, c, m)
                        nc.vector.memset(acc[C:2 * C, 0:KH - 1, c * P:(c + m) * P], 0.0).then_inc(s_clear, 1)
                    else:
                        if n == 0:
                            dve.wait_ge(s_hd, 16 * len(CHUNKS))
                        nc.vector.tensor_tensor(y, rows, x_rows[:, c:c + m, :], ALU.add).then_inc(s_hr, 1)
                        dve.wait_ge(s_hr, d + 1)
                        spread = lambda a: a.rearrange("p (j o) -> p j o", o=1).broadcast_to([P, m, C])
                        link(nc.vector.tensor_reduce(ysum[:, c:c + m], y, AX, ALU.add))
                        link(nc.vector.tensor_scalar(ysum[:, c:c + m], ysum[:, c:c + m], -1.0 / C, None, ALU.mult))
                        link(nc.vector.tensor_tensor(y, y, spread(ysum[:, c:c + m]), ALU.add))
                        link(nc.vector.tensor_tensor(ysq[:, 0:m, :], y, y, ALU.mult))
                        link(nc.vector.tensor_reduce(yvar[:, c:c + m], ysq[:, 0:m, :], AX, ALU.add))
            nc.vector.memset(mark[:], 0.0).then_inc(s_var, 1)
            dve.wait_ge(s_std, 1)
            link(nc.vector.reciprocal(yrstd[:], ystd[:]))
            nc.vector.tensor_tensor(h_rows[:], h_rows[:],
                                    yrstd[:].rearrange("p (j o) -> p j o", o=1).broadcast_to([P, NB, C]),
                                    ALU.mult).then_inc(s_fin, 1)


_INS = ['x', 'src', 'dst', 'edge_attr_2', 'L0_gnn_W1', 'L0_gnn_root1', 'L0_gnn_b1', 'L0_gnn_W2', 'L0_gnn_root2',
        'L0_gnn_b2']


def kernel(**inputs):
    import numpy as _np
    import concourse.bacc as _bacc
    from concourse import mybir as _mybir
    from concourse.bass_utils import run_bass_kernel_spmd as _run

    nc = _bacc.Bacc("TRN2", target_bir_lowering=False, num_devices=1)
    arrays, args = {}, []
    for name in _INS:
        a = _np.ascontiguousarray(inputs[name])
        arrays[f"in_{name}_dram"] = a
        args.append(nc.dram_tensor(f"in_{name}_dram", a.shape, _mybir.dt.from_np(a.dtype), kind="ExternalInput").ap())
    out = nc.dram_tensor("out_0_dram", (3125, 64), _mybir.dt.float32, kind="ExternalOutput").ap()
    spline_gnn_program(nc, *args, out)
    r = _run(nc, [arrays], core_ids=[0])
    return r.results[0]["out_0_dram"]
```

```python
import concourse.bass as bass
from concourse import mybir
from contextlib import ExitStack


def spline_gnn_program(nc, x, src, dst, attr, W1, root1, b1, W2, root2, b2, out):
    fp32 = mybir.dt.float32
    i32 = mybir.dt.int32
    i16 = mybir.dt.int16
    fp16 = mybir.dt.float16
    bf16 = mybir.dt.bfloat16
    ALU = mybir.AluOpType
    ACT = mybir.ActivationFunctionType
    AX = mybir.AxisListType.X
    DVE_ONLY = [mybir.EngineType.DVE]

    NODES, C = x.shape
    EDGES = src.shape[0]
    K = W1.shape[0]
    KH = (K + 1) // 2
    EPS = 1e-5

    P = 125
    E = 128
    SIZES = [4, 4, 3, 3]
    G = len(SIZES)
    START = [sum(SIZES[:g]) for g in range(G)]
    BT = sum(SIZES)
    R = 4
    DT = BT - R
    DMA_TILES = [min(SIZES[g], max(0, DT - START[g])) for g in range(G)]
    LAST_DMA = max(g for g in range(G) if DMA_TILES[g])
    PAIRS = -(-EDGES // (E * 2 * BT))
    BODIES = PAIRS * 2
    T = BODIES * BT
    NB = NODES // P
    FIFTHS, NQ = 5, NB // 5
    ROWS = 98
    RG = T // ROWS
    FULL = EDGES // (RG * E)
    TAIL = EDGES - FULL * RG * E
    PADS = FULL // 32 * 32
    W = 8
    WG = 100
    WINDOWS = -(-NODES // WG)
    NPAD = WINDOWS * WG
    FAR = 65536.0
    MID = NODES // 2
    CB = 4
    CHUNKS = [(c, min(CB, NB - c)) for c in range(0, NB, CB)]
    LAYERS = [(W1, root1, b1), (W2, root2, b2)]
    assert NODES - MID + P <= 2048 and NB * P == NODES and NB % FIFTHS == 0 and RG * ROWS == T
    assert 0 < TAIL and FULL == ROWS - 1 and EDGES % E % 32 == 0

    ctx = ExitStack()
    with ctx:
        def sb(name, shape, dt=fp32):
            return ctx.enter_context(nc.sbuf_tensor(name, shape, dt))

        def pb(name, shape):
            return ctx.enter_context(nc.psum_tensor(name, shape, fp32))

        def sem(name):
            return ctx.enter_context(nc.semaphore(name))

        h_dram = nc.dram_tensor("h_dram", (NODES, C), fp32, kind="Internal").ap()
        src16_dram = nc.dram_tensor("src16_dram", (T * E,), fp16, kind="Internal").ap()
        base_dram = nc.dram_tensor("base_dram", (T,), i32, kind="Internal").ap()

        PICKED = NB * R * E // 2
        GEN_WORDS = NPAD // 2 + (2 * KH + 1) * WG + C
        stage = sb("stage", [128, PICKED + 2 * 3 * T])
        row_table = lambda n: stage[0:ROWS, n * RG * E:(n + 1) * RG * E]
        by_tile = lambda a: a.rearrange("r (g p) -> r g p", p=E)
        src_rows = row_table(0).bitcast(i32)
        dst_rows = row_table(1).bitcast(i32)
        src_i, dst_i = by_tile(src_rows), by_tile(dst_rows)
        src_f = by_tile(row_table(2))
        dst_f = by_tile(row_table(3))
        rel_f = by_tile(row_table(4))
        near_f = by_tile(row_table(5))
        pick = stage[0:P, 0:PICKED].bitcast(bf16).rearrange("p (j e) -> p j e", e=R * E)
        attr_rows = stage[0:ROWS, PICKED + 2 * 3 * T - 2 * RG * E:]
        attr_r = attr_rows.rearrange("r (g p v) -> r g p v", p=E, v=2)
        quad = stage[0:E, PICKED:].rearrange("p (v n t) -> p v n t", v=2, n=3)
        gen_room = stage[0:E, PICKED:PICKED + GEN_WORDS]
        iotaN = gen_room[:, 0:NPAD // 2].bitcast(i16)
        gen_rhs = gen_room[:, NPAD // 2:NPAD // 2 + 2 * KH * WG].rearrange("p (k w) -> p k w", w=WG)
        gen_hot = gen_room[:, NPAD // 2 + 2 * KH * WG:NPAD // 2 + (2 * KH + 1) * WG]
        gen_x = gen_room[:, NPAD // 2 + (2 * KH + 1) * WG:NPAD // 2 + (2 * KH + 1) * WG + C]
        mark = sb("mark", [1, 1])
        src_16 = sb("src_16", [ROWS, RG, E], fp16)
        base_f = sb("base_f", [ROWS, RG])
        base_i = sb("base_i", [ROWS, RG], i32)
        far_col = sb("far_col", [ROWS, 1])
        far_one = sb("far_one", [1, 1])
        flag_i = sb("flag_i", [1, 1], i32)
        base_row = sb("base_row", [1, T], i32)
        srcT = sb("srcT", [E, T])
        relT = sb("relT", [E, T + BT])
        farT = sb("farT", [E, T])
        basis = sb("basis", [E, T + BT, 2 * KH])
        ident = sb("ident", [128, 128])
        window_i = sb("window_i", [E, W], i16)
        zero = sb("zero", [128, 1])
        plus_root = sb("plus_root", [E, 1])
        minus_half = sb("minus_half", [E, 1])
        wst = [sb(f"wst{l}", [128, KH, C]) for l in range(2)]
        bias = [sb(f"bias{l}", [128, 1]) for l in range(2)]
        x_rows = sb("x_rows", [P, NB, C])
        h_rows = sb("h_rows", [P, NB, C])
        acc = sb("acc", [128, KH, NPAD])
        idx = sb("idx", [E, 2, DT], i32)
        xg = sb("xg", [E, BT, C])
        hot = sb("hot", [E, BT, W])
        rhs = sb("rhs", [E, BT, K, W])
        src_b = sb("src_b", [P, 2, R * E], fp16)
        src_p = sb("src_p", [P, R * E], fp16)
        lane = sb("lane", [P, 1])
        parts = sb("parts", [P, NB, 3, C], bf16)
        rest = sb("rest", [P, 2, CB, C])
        gen_idx = sb("gen_idx", [E, 1], i32)
        ysum = sb("ysum", [P, NB])
        ysq = sb("ysq", [P, 2, CB, C])
        yvar = sb("yvar", [P, NB])
        ystd = sb("ystd", [P, NB])
        yrstd = sb("yrstd", [P, NB])
        eps = sb("eps", [P, 1])

        bank = pb("bank", [128, 8, 512])
        ps_p = [bank[:, 2 * i:2 * i + 2].rearrange("p b (h c) -> p (b h) c", h=2) for i in range(2)]
        ps_e = [bank[:, 4 + g] for g in range(G)]
        ps_d = [bank[:, i] for i in range(4)]
        ps_t = [bank[:, 4 + i] for i in range(4)]
        ps_g = ps_e[3]

        s_pads = sem("s_pads")
        s_src = sem("s_src")
        s_dst = sem("s_dst")
        s_attr = sem("s_attr")
        s_x = sem("s_x")
        s_w = sem("s_w")
        s_const = sem("s_const")
        s_zero = sem("s_zero")
        s_zero_up = sem("s_zero_up")
        s_bias = sem("s_bias")
        s_quad = sem("s_quad")
        s_shared = sem("s_shared")
        s_rows = sem("s_rows")
        s_dve = sem("s_dve")
        s_tr = sem("s_tr")
        s_ev = sem("s_ev")
        s_base_w = sem("s_base_w")
        s_base_r = sem("s_base_r")
        s_far = sem("s_far")
        s_flagT = sem("s_flagT")
        s_flag = sem("s_flag")
        s_hi = sem("s_hi")
        s_rest = sem("s_rest")
        s_middle = sem("s_middle")
        s_idx = [sem(f"s_idx{i}") for i in range(2)]
        s_gather = [sem(f"s_gather{i}") for i in range(G)]
        s_src16 = sem("s_src16")
        s_src_b = [sem(f"s_src_b{i}") for i in range(2)]
        s_pick = sem("s_pick")
        s_used = sem("s_used")
        s_kept = sem("s_kept")
        s_picked = sem("s_picked")
        s_lane = sem("s_lane")
        s_mid = sem("s_mid")
        s_parts = sem("s_parts")
        s_blank = sem("s_blank")
        s_go = sem("s_go")
        s_hot = sem("s_hot")
        s_rhs = [sem(f"s_rhs{i}") for i in range(G)]
        s_mm = [sem(f"s_mm{i}") for i in range(G)]
        s_add = sem("s_add")
        s_acc = sem("s_acc")
        s_iota = sem("s_iota")
        s_gi = [sem(f"s_gi{i}") for i in range(2)]
        s_gx = [sem(f"s_gx{i}") for i in range(2)]
        s_gh = [sem(f"s_gh{i}") for i in range(2)]
        s_gr = [sem(f"s_gr{i}") for i in range(2)]
        s_gm = [sem(f"s_gm{i}") for i in range(2)]
        s_ga = [sem(f"s_ga{i}") for i in range(2)]
        s_dense = sem("s_dense")
        s_hr = sem("s_hr")
        s_relu = sem("s_relu")
        s_ht = sem("s_ht")
        s_hd = sem("s_hd")
        s_clear = sem("s_clear")
        s_cent = sem("s_cent")
        s_sq = sem("s_sq")
        s_var = sem("s_var")
        s_std = sem("s_std")
        s_rstd = sem("s_rstd")
        s_fin = sem("s_fin")
        s_out = sem("s_out")

        block = ctx.enter_context(nc.Block())

        node_view = lambda a: a.rearrange("(j p) c -> p j c", p=P)
        HALF = RG // 2
        BATCHES = [(n, h) for n in ("src", "v0", "v1", "rel", "far") for h in range(2)] + \
                  [("x", c) for c in range(len(CHUNKS))]
        SRC, V, TABLES, NBATCH = 2, 6, 10, len(BATCHES)
        SRC_F, SRC_16, BASE_I, REL_F, FAR_F = range(1, 6)

        @block.sync
        def _(sp):
            def load_list(rows, flat, v, done, a, b, n):
                at = v * RG * E * a
                sp.dma_start(rows[a:b, 0:v * n],
                             flat[at:at + (b - a) * v * n].rearrange("(r e) -> r e", e=v * n)).then_inc(done, 16)

            lists = [(src_rows, src, 1, s_src), (dst_rows, dst, 1, s_dst),
                     (attr_rows, attr.rearrange("e v -> (e v)"), 2, s_attr)]
            for one in lists[0:2]:
                load_list(*one, 0, PADS, RG * E)
            for i, one in enumerate(lists):
                if i == 2:
                    load_list(*one, 0, PADS, RG * E)
                sp.wait_ge(s_pads, i + 1)
                load_list(*one, PADS, FULL, RG * E)
                load_list(*one, FULL, ROWS, TAIL)
            sp.dma_start(x_rows[:], node_view(x)).then_inc(s_x, 16)
            for l, (Wl, root, b) in enumerate(LAYERS):
                sp.dma_start(wst[l][0:C], Wl[0:KH].rearrange("k c o -> c k o")).then_inc(s_w, 16)
                sp.dma_start(wst[l][C:2 * C, 0:K - KH], Wl[KH:K].rearrange("k c o -> c k o")).then_inc(s_w, 16)
                sp.dma_start(wst[l][C:2 * C, K - KH], root).then_inc(s_w, 16)
                sp.dma_start(bias[l][C:2 * C, :], b.rearrange("(c o) -> c o", o=1)).then_inc(s_w, 16)
            sp.wait_ge(s_rows, SRC_16)
            sp.dma_start(src16_dram.rearrange("(r g p) -> r g p", r=ROWS, p=E), src_16[:]).then_inc(s_src16, 16)
            sp.wait_ge(s_rows, BASE_I)
            sp.dma_start(base_dram.rearrange("(r g) -> r g", r=ROWS), base_i[:]).then_inc(s_base_w, 16)

            def load_sources(slot, body):
                edges = src16_dram.rearrange("(o e) -> o e", o=1)[:, bass.ds(body * (BT * E) + DT * E, R * E)]
                sp.dma_start(src_b[:, slot, :], edges.broadcast_to([P, R * E])).then_inc(s_src_b[slot], 16)

            def load_loop(l):
                with sp.Fori(0, PAIRS - 1) as j:
                    for b in range(2):
                        sp.wait_ge(s_lane, j * 2 + (l * BODIES + b + 1))
                        load_sources(b, j * 2 + (b + 2))

            sp.wait_ge(s_src16, 16)
            for b in range(2):
                load_sources(b, b)
            sp.wait_ge(s_base_w, 16)
            sp.dma_start(base_row[:], base_dram.rearrange("(o t) -> o t", o=1)).then_inc(s_base_r, 16)
            load_loop(0)
            for b in range(2):
                sp.wait_ge(s_lane, BODIES + b - 1)
                load_sources(b, b)
            for n, (c, m) in enumerate(CHUNKS):
                sp.wait_ge(s_hr, n + 1)
                sp.dma_start(node_view(h_dram)[:, c:c + m, :], h_rows[:, c:c + m, :]).then_inc(s_hd, 16)
            sp.wait_ge(s_hd, 16 * len(CHUNKS))
            load_loop(1)
            for n, (c, m) in enumerate(CHUNKS):
                sp.wait_ge(s_fin, n + 1)
                sp.dma_start(node_view(out)[:, c:c + m, :], h_rows[:, c:c + m, :]).then_inc(s_out, 16)
            sp.wait_ge(s_out, 16 * len(CHUNKS))

        def make_basis(eng, i, first, end):
            k3 = basis[:, first:end, 3 * i:3 * i + 3].rearrange("p t k -> p k t")
            one = quad[:, 0, i:i + 1, first:end].broadcast_to([E, 3, end - first])
            return eng.tensor_tensor(k3, one, quad[:, 1, :, first:end], ALU.mult)

        @block.gpsimd
        def _(pool):
            nc.gpsimd.memset(ident[:], 0.0).then_inc(s_const, 1)
            pool.wait_ge(s_const, 1)
            nc.gpsimd.affine_select(out=ident[:], in_=ident[:], compare_op=ALU.not_equal, fill=1.0, base=0,
                                    pattern=[[-1, 128]], channel_multiplier=1).then_inc(s_const, 1)
            nc.gpsimd.iota(window_i[:], pattern=[[1, W]], base=0, channel_multiplier=0,
                           allow_small_or_imprecise_dtypes=True)
            nc.gpsimd.iota(lane[:], pattern=[[0, 1]], base=0, channel_multiplier=1,
                           allow_small_or_imprecise_dtypes=True).then_inc(s_const, 1)
            pool.wait_ge(s_const, 3)
            nc.gpsimd.memset(acc[0:C], 0.0).then_inc(s_zero, 1)
            pool.wait_ge(s_zero, 1)
            nc.gpsimd.memset(acc[C:2 * C, KH - 1, NODES:NPAD], 0.0).then_inc(s_zero, 1)
            for l in range(2):
                table = (x, h_dram)[l]
                if l == 1:
                    for n, (c, m) in enumerate(CHUNKS):
                        pool.wait_ge(s_dense, n + 1)
                        nc.gpsimd.memset(acc[0:C, :, c * P:(c + m) * P], 0.0).then_inc(s_clear, 1)
                    pool.wait_ge(s_hd, 16 * len(CHUNKS))

                def gather_body(j, b):
                    for g in range(G):
                        if DMA_TILES[g] == 0:
                            continue
                        if g == 0:
                            pool.wait_ge(s_idx[b], j + (l * PAIRS + 1))
                        pool.wait_ge(s_mm[g], j * 2 + (l * BODIES + b + 1))
                        pool.sem_inc(s_go, 1)
                        for t in range(START[g], START[g] + DMA_TILES[g]):
                            pool.indirect_dma_start(xg[:, t, :], None, table,
                                                    bass.IndirectOffsetOnAxis(idx[:, b, t:t + 1], 0),
                                                    ).then_inc(s_gather[g], 16)

                gather_body(0, 0)
                if l == 0:
                    pool.wait_ge(s_quad, 1)
                    pool.wait_ge(s_zero, 2)
                    make_basis(nc.gpsimd, 2, BT, T).then_inc(s_shared, 1)
                gather_body(0, 1)
                with pool.Fori(1, PAIRS) as j:
                    for b in range(2):
                        gather_body(j, b)
                if l == 0:
                    pool.wait_ge(s_flag, 1)
                    general = pool.value_load(flag_i[0:1, 0:1], min_val=0, max_val=1)
                with pool.If(general):
                    if l == 0:
                        pool.wait_ge(s_rhs[0], 2)
                        nc.gpsimd.iota(iotaN, pattern=[[1, NPAD]], base=0, channel_multiplier=0,
                                       allow_small_or_imprecise_dtypes=True).then_inc(s_iota, 1)
                    with pool.Fori(0, T) as t:
                        pool.wait_ge(s_gi[l], t + 1)
                        pool.sem_inc(s_go, 1)
                        pool.indirect_dma_start(gen_x, None, table,
                                                bass.IndirectOffsetOnAxis(gen_idx[:, 0:1], 0),
                                                ).then_inc(s_gx[l], 16)
            for n, (c, m) in enumerate(CHUNKS):
                y = h_rows[:, c:c + m, :]
                pool.wait_ge(s_rstd, n + 1)
                if n:
                    pool.wait_ge(s_fin, n)
                scale = yrstd[:, c:c + m].rearrange("p (j o) -> p j o", o=1).broadcast_to([P, m, C])
                nc.gpsimd.tensor_tensor(y, y, scale, ALU.mult).then_inc(s_fin, 1)

        @block.scalar
        def _(act):
            def evacuate(n):
                kind, h = BATCHES[n]
                ps = ps_d[n % 4]
                act.wait_ge(s_tr, n + 1)
                if kind == "x":
                    c, m = CHUNKS[h]
                    nc.scalar.copy(acc[C:2 * C, KH - 1, c * P:(c + m) * P], ps[0:C, 0:m * P]).then_inc(s_ev, 1)
                    return
                half = lambda table: table.rearrange("p (r g) -> p g r", g=RG)[:, h * HALF:(h + 1) * HALF, :]
                tiles = ps[0:E, 0:HALF * ROWS].rearrange("p (g r) -> p g r", g=HALF)
                if kind[0] == "v":
                    q = quad[:, int(kind[1])]
                    nc.scalar.activation(half(q[:, 2]), tiles, ACT.Square, scale=0.5 ** 0.5)
                    nc.scalar.activation(half(q[:, 0]), tiles, ACT.Square, bias=plus_root[:], scale=-0.5 ** 0.5)
                    nc.scalar.activation(half(q[:, 1]), tiles, ACT.Square, bias=minus_half[:]).then_inc(s_ev, 1)
                else:
                    to = {"src": srcT[:], "rel": relT[:, 0:T], "far": farT[:]}[kind]
                    nc.scalar.copy(half(to), tiles).then_inc(s_ev, 1)

            def place_indices(slot, body):
                nc.scalar.copy(idx[:, slot], srcT[:, bass.ds(body * BT, DT)]).then_inc(s_idx[slot], 1)

            def keep_rows(n):
                c, m = CHUNKS[n]
                rows = ps_t[n % 4][0:P, 0:m * C].rearrange("p (j c) -> p j c", c=C)
                act.wait_ge(s_ht, n + 1)
                nc.scalar.copy(h_rows[:, c:c + m, :], rows).then_inc(s_hr, 1)
                split_high(rows, c, m)

            def square(n):
                c, m = CHUNKS[n]
                act.wait_ge(s_cent, n + 1)
                nc.scalar.square(ysq[:, n % 2, 0:m, :], h_rows[:, c:c + m, :]).then_inc(s_sq, 1)

            def deviation(n):
                c, m = CHUNKS[n]
                act.wait_ge(s_var, n + 1)
                nc.scalar.activation(ystd[:, c:c + m], yvar[:, c:c + m], ACT.Sqrt, bias=eps[:],
                                     scale=1.0 / C).then_inc(s_std, 1)

            def keep_picked(slot, body):
                act.wait_ge(s_used, body * FIFTHS + FIFTHS)
                act.wait_ge(s_mm[G - 1], body + 1)
                nc.scalar.copy(xg[:, DT:BT], ps_p[slot][:, :, 0:C]).then_inc(s_kept, 1)

            def split_high(rows, c, m):
                nc.scalar.copy(parts[:, c:c + m, 0, :], rows).then_inc(s_hi, 1)

            def split_middle(left, c, m, n):
                act.wait_ge(s_rest, n + 1)
                nc.scalar.copy(parts[:, c:c + m, 1, :], left).then_inc(s_middle, 1)

            for n in range(SRC):
                evacuate(n)
            act.wait_ge(s_ev, SRC)
            for b in range(2):
                place_indices(b, b)
            act.wait_ge(s_bias, 1)
            for n in range(SRC, V):
                if BATCHES[n] == ("v1", 0):
                    act.wait_ge(s_x, 16)
                    split_high(x_rows[:], 0, NB)
                    act.wait_ge(s_tr, V)
                evacuate(n)
            split_middle(h_rows[:], 0, NB, 0)
            for n in range(V, NBATCH):
                evacuate(n)
            nc.scalar.copy(acc[C:2 * C, 0:KH - 1], zero[C:2 * C, :].rearrange("c (k n) -> c k n", k=1).broadcast_to(
                [C, KH - 1, NPAD])).then_inc(s_zero_up, 1)
            for l in range(2):
                keep_picked(0, l * BODIES)
                with act.Fori(0, PAIRS - 1) as j:
                    for b in range(2):
                        act.wait_ge(s_mm[LAST_DMA], j * 2 + (l * BODIES + b + 2))
                        place_indices(b, j * 2 + (b + 2))
                        keep_picked(1 - b, j * 2 + (l * BODIES + b + 1))
                keep_picked(1, (l + 1) * BODIES - 1)
                if l == 0:
                    for b in range(2):
                        act.wait_ge(s_mm[LAST_DMA], BODIES + b)
                        place_indices(b, b)
                if l == 0:
                    act.wait_ge(s_ev, NBATCH)
                    act.wait_ge(s_flag, 1)
                    general = act.value_load(flag_i[0:1, 0:1], min_val=0, max_val=1)
                with act.If(general):
                    with act.Fori(0, T) as t:
                        nc.scalar.copy(gen_idx[:], srcT[:, bass.ds(t, 1)]).then_inc(s_gi[l], 1)
                        act.wait_ge(s_gm[l], t * WINDOWS + WINDOWS)
                if l == 0:
                    act.wait_ge(s_w, 16 * 8)
                for n in range(len(CHUNKS) + 2):
                    if n < len(CHUNKS):
                        c, m = CHUNKS[n]
                        act.wait_ge(s_dense, l * len(CHUNKS) + n + 1)
                        nc.scalar.activation(acc[C:2 * C, KH - 1, c * P:(c + m) * P],
                                             ps_d[n % 4][C:2 * C, 0:m * P], ACT.Relu,
                                             bias=bias[l][C:2 * C, :]).then_inc(s_relu, 1)
                    if l == 0:
                        if 1 <= n <= len(CHUNKS):
                            keep_rows(n - 1)
                        if n >= 2:
                            c, m = CHUNKS[n - 2]
                            split_middle(rest[:, n % 2, 0:m, :], c, m, n - 1)
                    else:
                        if 1 <= n <= len(CHUNKS):
                            square(n - 1)
                        if n >= 2:
                            deviation(n - 2)

        def turn_back(pe, l, n):
            c, m = CHUNKS[n]
            pe.wait_ge(s_relu, l * len(CHUNKS) + n + 1)
            if n >= 4:
                pe.wait_ge((s_hi, s_hr)[l], l * len(CHUNKS) + n - 4 + (2, 1)[l])
            for j in range(m):
                last = nc.tensor.transpose(ps_t[n % 4][0:P, j * C:(j + 1) * C],
                                           acc[C:2 * C, KH - 1, (c + j) * P:(c + j + 1) * P],
                                           ident[C:2 * C, C:2 * C])
            last.then_inc(s_ht, 1)

        @block.tensor
        def _(pe):
            for g in range(G):
                pe.sem_inc(s_mm[g], 1)
            pe.sem_inc(s_picked, 1)
            pe.wait_ge(s_const, 2)
            for n, (kind, h) in enumerate(BATCHES):
                if n == TABLES:
                    pe.wait_ge(s_far, 1)
                    nc.tensor.transpose(ps_g[0:1, 0:ROWS], far_col[:], ident[0:ROWS, 0:ROWS]).then_inc(s_flagT, 1)
                if n >= 4:
                    pe.wait_ge(s_ev, n - 4 + 1)
                if kind == "src":
                    pe.wait_ge(s_rows, SRC_F)
                elif kind == "rel":
                    pe.wait_ge(s_rows, REL_F)
                elif kind == "far":
                    pe.wait_ge(s_rows, FAR_F)
                elif kind == "x":
                    pe.wait_ge(s_x, 16)
                else:
                    pe.wait_ge(s_attr, 48)
                ps = ps_d[n % 4]
                if kind == "x":
                    c, m = CHUNKS[h]
                    for j in range(m):
                        last = nc.tensor.transpose(ps[0:C, j * P:(j + 1) * P], x_rows[:, c + j, :],
                                                   ident[0:P, 0:P])
                else:
                    for j in range(HALF):
                        g = h * HALF + j
                        rows = {"src": src_f, "rel": rel_f, "far": dst_f}[kind][:, g, :] if kind[0] != "v" \
                            else attr_r[:, g, :, int(kind[1])]
                        last = nc.tensor.transpose(ps[0:E, j * ROWS:(j + 1) * ROWS], rows,
                                                   ident[0:ROWS, 0:ROWS])
                last.then_inc(s_tr, 1)
            pe.wait_ge(s_ev, NBATCH)
            for l in range(2):
                if l == 1:
                    pe.wait_ge(s_hi, len(CHUNKS) + 1)
                pe.wait_ge(s_parts, l * len(CHUNKS) + 1)

                def pick_fifth(slot, body, q):
                    pe.wait_ge(s_pick, body * FIFTHS + (q + 1))
                    for j in range(q * NQ, (q + 1) * NQ):
                        for r in range(R):
                            last = nc.tensor.matmul(
                                ps_p[slot][:, r, 0:3 * C], pick[:, j, r * E:(r + 1) * E],
                                parts[:, j].rearrange("p n c -> p (n c)"),
                                start=(j == 0 and r % 2 == 0), stop=(j == NB - 1 and (r % 2 == 1 or r == R - 1)))
                    last.then_inc(s_used, 1)

                def multiply(g, i, b):
                    body = i * 2 + (l * BODIES + b)
                    pe.wait_ge(s_rhs[g], body + 1)
                    if DMA_TILES[g]:
                        pe.wait_ge(s_gather[g], body * (16 * DMA_TILES[g]) + 16 * DMA_TILES[g])
                    for u in range(SIZES[g]):
                        t = START[g] + u
                        if t == DT:
                            pe.wait_ge(s_picked, body + 2)
                        for cols, ks in ((slice(0, C), slice(0, KH)), (slice(C, 2 * C), slice(KH, K))):
                            n = (ks.stop - ks.start) * W
                            last = nc.tensor.matmul(ps_e[g][cols, u * KH * W:u * KH * W + n], xg[:, t, :],
                                                    rhs[:, t, ks, :], start=True, stop=True)
                    last.then_inc(s_mm[g], 1)

                def run_body(i, b, pick_next=True, products_first=False):
                    body = i * 2 + (l * BODIES + b)
                    for g in range(G):
                        if products_first:
                            multiply(g, i, b)
                        if pick_next:
                            if g == 0:
                                pe.wait_ge(s_picked, body + 1)
                            pick_fifth(1 - b, body + 1, g)
                        if not products_first:
                            multiply(g, i, b)
                    if pick_next:
                        pick_fifth(1 - b, body + 1, G)

                for q in range(FIFTHS):
                    pick_fifth(0, l * BODIES, q)
                pe.wait_ge(s_blank, l + 1)
                if l == 0:
                    pe.wait_ge(s_flag, 1)
                run_body(0, 0, products_first=True)
                run_body(0, 1)
                with pe.Fori(1, PAIRS - 1) as i:
                    for b in range(2):
                        run_body(i, b)
                run_body(PAIRS - 1, 0)
                run_body(PAIRS - 1, 1, pick_next=False)
                if l == 0:
                    general = pe.value_load(flag_i[0:1, 0:1], min_val=0, max_val=1)
                with pe.If(general):
                    with pe.Fori(0, T) as t:
                        with pe.Fori(0, WINDOWS) as w:
                            pe.wait_ge(s_gx[l], t * 16 + 16)
                            pe.wait_ge(s_gr[l], t * WINDOWS + w + 1)
                            for half in range(2):
                                last = nc.tensor.matmul(ps_g[half * C:(half + 1) * C, 0:KH * WG], gen_x,
                                                        gen_rhs[:, half * KH:(half + 1) * KH, :],
                                                        start=True, stop=True)
                            last.then_inc(s_gm[l], 1)
                pe.wait_ge(s_acc, l + 1)
                if l == 0:
                    pe.wait_ge(s_w, 16 * 8)
                for n, (c, m) in enumerate(CHUNKS):
                    if n >= 4:
                        pe.wait_ge(s_relu, l * len(CHUNKS) + n - 4 + 1)
                    for k in range(KH):
                        last = nc.tensor.matmul(ps_d[n % 4][C:2 * C, 0:m * P], wst[l][:, k, :],
                                                acc[:, k, c * P:(c + m) * P], start=(k == 0), stop=(k == KH - 1))
                    last.then_inc(s_dense, 1)
                    if n:
                        turn_back(pe, l, n - 1)
                turn_back(pe, l, len(CHUNKS) - 1)

        @block.vector
        def _(dve):
            chain = [0]

            def link(ins):
                chain[0] += 1
                ins.then_inc(s_dve, 1)
                dve.wait_ge(s_dve, chain[0])

            nc.vector.memset(src_rows[PADS:ROWS, TAIL:], 0).then_inc(s_pads, 1)
            nc.vector.memset(dst_rows[PADS:ROWS, TAIL:], NODES - 1).then_inc(s_pads, 1)
            nc.vector.memset(attr_rows[PADS:ROWS, 2 * TAIL:], 0.0).then_inc(s_pads, 1)
            nc.vector.memset(eps[:], EPS)
            nc.vector.memset(zero[:], 0.0)
            nc.vector.memset(plus_root[:], 0.5 ** 0.5)
            nc.vector.memset(minus_half[:], -0.5).then_inc(s_bias, 1)
            dve.sem_inc(s_add, 1)
            nc.vector.memset(basis[:, :, K:2 * KH], 0.0)
            link(nc.vector.memset(src_p[:], FAR / 4))
            dve.wait_ge(s_src, 48)
            nc.vector.tensor_copy(src_f, src_i).then_inc(s_rows, 1)
            nc.vector.tensor_scalar(src_16[:], src_i, float(MID), None, ALU.subtract).then_inc(s_rows, 1)
            dve.wait_ge(s_dst, 48)
            link(nc.vector.tensor_copy(dst_f, dst_i))
            link(nc.vector.tensor_reduce(base_f[:], dst_f, AX, ALU.min))
            nc.vector.tensor_copy(base_i[:], base_f[:]).then_inc(s_rows, 1)
            base_b = base_f[:].rearrange("r (g o) -> r g o", o=1).broadcast_to([ROWS, RG, E])
            nc.vector.tensor_tensor(rel_f, dst_f, base_b, ALU.subtract).then_inc(s_rows, 1)
            dve.wait_ge(s_rows, REL_F)
            link(nc.vector.tensor_scalar(near_f, rel_f, float(W), FAR, ALU.is_lt, ALU.mult))
            nc.vector.tensor_tensor(dst_f, dst_f, near_f, ALU.add).then_inc(s_rows, 1)
            nc.vector.tensor_reduce(far_col[:], rel_f.rearrange("r g p -> r (g p)"), AX, ALU.max).then_inc(s_far, 1)

            def split_rest(rows, left, c, m, n):
                dve.wait_ge(s_hi, n + 1)
                nc.vector.tensor_tensor(left, rows, parts[:, c:c + m, 0, :], ALU.subtract).then_inc(s_rest, 1)

            def split_low(left, c, m, n):
                dve.wait_ge(s_middle, n + 1)
                nc.vector.tensor_tensor(parts[:, c:c + m, 2, :], left, parts[:, c:c + m, 1, :],
                                        ALU.subtract).then_inc(s_parts, 1)

            def sources_by_lane(slot):
                nc.vector.tensor_scalar(src_p[:], src_b[:, slot], lane[:], None,
                                        ALU.subtract).then_inc(s_lane, 1)

            def pick_block(j):
                return nc.vector.tensor_scalar(pick[:, j, :], src_p[:], float(P * j - MID), None, ALU.is_equal)

            def make_fifth(q):
                for j in range(q * NQ, (q + 1) * NQ):
                    last = pick_block(j)
                last.then_inc(s_pick, 1)

            def make_hot(tile):
                rel = relT[:, bass.ds(tile, BT)].rearrange("p (t o) -> p t o", o=1)
                window = window_i[:].rearrange("p (t w) -> p t w", t=1)
                nc.vector.tensor_tensor(hot[:], window.broadcast_to([E, BT, W]), rel.broadcast_to([E, BT, W]),
                                        ALU.is_equal).then_inc(s_hot, 1)

            def make_rhs(g, body_tile):
                n, mine = SIZES[g], slice(START[g], START[g] + SIZES[g])
                bs = basis[:, bass.ds(body_tile + START[g], n), 0:K]
                nc.vector.tensor_tensor(
                    rhs[:, mine], bs.rearrange("p u (k o) -> p u k o", o=1).broadcast_to([E, n, K, W]),
                    hot[:, mine].rearrange("p u (o w) -> p u o w", o=1).broadcast_to([E, n, K, W]),
                    ALU.mult).then_inc(s_rhs[g], 1)

            def blank_slots():
                for g in range(G):
                    slots = ps_e[g][C:2 * C, 0:max(SIZES) * KH * W].rearrange("c (u k w) -> c u k w", k=KH, w=W)
                    last = nc.vector.memset(slots[:, :, K - KH, :], 0.0)
                last.then_inc(s_blank, 1)

            blank_slots()
            dve.wait_ge(s_x, 16)
            split_rest(x_rows[:], h_rows[:], 0, NB, 0)
            dve.wait_ge(s_ev, V)
            nc.vector.tensor_scalar(quad[:, :, 1, :], quad[:, :, 1, :], -1.0, 0.75, ALU.mult,
                                    ALU.add).then_inc(s_quad, 1)
            dve.wait_ge(s_quad, 1)
            for i in range(3):
                last = make_basis(nc.vector, i, 0, BT)
            link(last)
            dve.wait_ge(s_const, 3)
            dve.wait_ge(s_src_b[0], 16)
            sources_by_lane(0)
            dve.wait_ge(s_lane, 1)
            dve.wait_ge(s_tr, TABLES)
            make_fifth(0)
            split_low(h_rows[:], 0, NB, 0)
            for q in range(1, FIFTHS):
                make_fifth(q)
            dve.wait_ge(s_flagT, 1)
            link(nc.vector.tensor_reduce(far_one[:], ps_g[0:1, 0:ROWS], AX, ALU.max))
            nc.vector.tensor_scalar(flag_i[:], far_one[:], float(W), None, ALU.is_ge).then_inc(s_flag, 1)
            dve.wait_ge(s_ev, TABLES)
            make_hot(0)
            dve.wait_ge(s_hot, 1)
            for g in range(G):
                make_rhs(g, 0)

            def finish_basis():
                for i in range(2):
                    last = make_basis(nc.vector, i, BT, T)
                link(last)
                dve.wait_ge(s_shared, 1)
                nc.vector.tensor_copy(basis[:, T:T + BT, :], basis[:, 0:BT, :])
                last_tile, used = EDGES // E, EDGES % E
                for a in range(used, E, 32):
                    nc.vector.memset(basis[a:a + 32, last_tile, :], 0.0)
                nc.vector.memset(basis[:, last_tile + 1:T, :], 0.0)
                link(nc.vector.tensor_copy(relT[:, T:T + BT], relT[:, 0:BT]))

            LATE = 2

            def clear(n):
                c, m = CHUNKS[n]
                dve.wait_ge(s_dense, n + 1)
                nc.vector.memset(acc[C:2 * C, 0:KH - 1, c * P:(c + m) * P], 0.0).then_inc(s_clear, 1)

            def chunk_rest(n):
                c, m = CHUNKS[n]
                if n >= 2:
                    dve.wait_ge(s_parts, n)
                dve.wait_ge(s_hr, n + 1)
                split_rest(h_rows[:, c:c + m, :], rest[:, n % 2, 0:m, :], c, m, n + 1)

            def chunk_low(n):
                c, m = CHUNKS[n]
                split_low(rest[:, n % 2, 0:m, :], c, m, n + 1)

            def run_body(i, b, l, next_rhs=True, next_pick=True, first=False):
                body = i * 2 + (l * BODIES + b)
                tile = i * (2 * BT) + b * BT

                _, at = nc.values_load_multi_w_load_instructions(
                    base_row[0:1, bass.ds(tile, BT)], engines=DVE_ONLY, min_val=0,
                    max_val=NODES - 1, skip_runtime_bounds_check_because="a destination is a node")

                def add_tile(g, u):
                    dve.wait_ge(s_add, body * BT + (START[g] + u + 1))
                    window = acc[:, :, bass.ds(at[START[g] + u], W)]
                    part = ps_e[g][:, u * KH * W:(u + 1) * KH * W].rearrange("c (k w) -> c k w", w=W)
                    nc.vector.tensor_tensor(window, window, part, ALU.add).then_inc(s_add, 1)

                dve.wait_ge(s_kept, body + 1)
                rows = xg[:, DT:BT]
                nc.vector.tensor_tensor(rows, rows, ps_p[b][:, :, C:2 * C], ALU.add).then_inc(s_mid, 1)
                if next_pick:
                    dve.wait_ge(s_src_b[b], i * 16 + 16 * (l * PAIRS + 1) + 16)
                    dve.wait_ge(s_pick, body * FIFTHS + 2 * FIFTHS)
                    sources_by_lane(b)
                dve.wait_ge(s_mid, body + 1)
                nc.vector.tensor_tensor(rows, rows, ps_p[b][:, :, 2 * C:3 * C], ALU.add).then_inc(s_picked, 1)
                for g in range(G):
                    if next_pick:
                        dve.wait_ge(s_used, body * FIFTHS + (FIFTHS + g + 1))
                        if g == 0:
                            dve.wait_ge(s_lane, body + 3)
                    dve.wait_ge(s_mm[g], body + 2)
                    for u in range(NQ):
                        if u < SIZES[g]:
                            add_tile(g, u)
                        if next_pick:
                            last = pick_block(g * NQ + u)
                    if next_pick:
                        last.then_inc(s_pick, 1)
                    if next_rhs:
                        if g == 0:
                            if first:
                                finish_basis()
                            dve.wait_ge(s_rhs[G - 1], body + 1)
                            make_hot(tile + BT)
                            dve.wait_ge(s_hot, body + 2)
                        make_rhs(g, tile + BT)
                if next_pick:
                    dve.wait_ge(s_used, body * FIFTHS + 2 * FIFTHS)
                    make_fifth(G)

            for l in range(2):
                if l == 1:
                    dve.wait_ge(s_hi, len(CHUNKS) + 1)
                    blank_slots()
                dve.wait_ge(s_src_b[1], 16 * (l * PAIRS + 1))
                dve.wait_ge(s_pick, (l * BODIES + 1) * FIFTHS)
                sources_by_lane(1)
                dve.wait_ge(s_lane, l * BODIES + 2)
                for q in range(FIFTHS):
                    dve.wait_ge(s_used, l * BODIES * FIFTHS + q + 1)
                    make_fifth(q)
                if l == 0:
                    dve.wait_ge(s_base_r, 16)
                    dve.wait_ge(s_zero_up, 1)
                    dve.wait_ge(s_zero, 2)
                    dve.wait_ge(s_ev, NBATCH)
                else:
                    dve.wait_ge(s_clear, 2 * len(CHUNKS))
                run_body(0, 0, l, first=(l == 0))
                run_body(0, 1, l)
                with dve.Fori(1, PAIRS - 1) as i:
                    for b in range(2):
                        run_body(i, b, l)
                if l == 0:
                    dve.wait_ge(s_flag, 1)
                    general = dve.value_load(flag_i[0:1, 0:1], min_val=0, max_val=1)
                run_body(PAIRS - 1, 0, l, next_pick=(l == 0))
                run_body(PAIRS - 1, 1, l, next_rhs=(l == 0), next_pick=False)
                dve.wait_ge(s_add, (l + 1) * T + 1)
                with dve.If(general):
                    dve.wait_ge(s_iota, 1)
                    with dve.Fori(0, T) as t:
                        b = basis[:, bass.ds(t, 1), :].rearrange("p o k -> p (o k)")
                        with dve.Fori(0, WINDOWS) as w:
                            nc.vector.tensor_scalar(gen_hot, iotaN[:, bass.ds(w * WG, WG)],
                                                    farT[:, bass.ds(t, 1)], None, ALU.is_equal).then_inc(s_gh[l], 1)
                            dve.wait_ge(s_gh[l], t * WINDOWS + w + 1)
                            nc.vector.tensor_tensor(
                                gen_rhs, b.rearrange("p (k o) -> p k o", o=1).broadcast_to([E, 2 * KH, WG]),
                                gen_hot.rearrange("p (o w) -> p o w", o=1).broadcast_to([E, 2 * KH, WG]),
                                ALU.mult).then_inc(s_gr[l], 1)
                            dve.wait_ge(s_gm[l], t * WINDOWS + w + 1)
                            window = acc[:, :, bass.ds(w * WG, WG)]
                            nc.vector.tensor_tensor(
                                window, window, ps_g[:, 0:KH * WG].rearrange("c (k w) -> c k w", w=WG), ALU.add,
                            ).then_inc(s_ga[l], 1)
                            dve.wait_ge(s_ga[l], t * WINDOWS + w + 1)
                nc.vector.memset(mark[:], 0.0).then_inc(s_acc, 1)
                if l == 0:
                    for n in range(len(CHUNKS) + 2):
                        if n < len(CHUNKS) - LATE:
                            clear(n)
                        if 1 <= n <= len(CHUNKS):
                            chunk_rest(n - 1)
                        if n >= 2:
                            chunk_low(n - 2)
                    for n in range(len(CHUNKS) - LATE, len(CHUNKS)):
                        clear(n)
            dve.wait_ge(s_hd, 16 * len(CHUNKS))

            def sum_squares(n):
                c, m = CHUNKS[n]
                dve.wait_ge(s_sq, n + 1)
                nc.vector.tensor_reduce(yvar[:, c:c + m], ysq[:, n % 2, 0:m, :], AX, ALU.add).then_inc(s_var, 1)

            def invert(n):
                c, m = CHUNKS[n]
                dve.wait_ge(s_std, n + 1)
                nc.vector.reciprocal(yrstd[:, c:c + m], ystd[:, c:c + m]).then_inc(s_rstd, 1)

            for n, (c, m) in enumerate(CHUNKS):
                y = h_rows[:, c:c + m, :]
                dve.wait_ge(s_ht, len(CHUNKS) + n + 1)
                nc.vector.tensor_tensor(y, ps_t[n % 4][0:P, 0:m * C].rearrange("p (j c) -> p j c", c=C),
                                        x_rows[:, c:c + m, :], ALU.add).then_inc(s_hr, 1)
                dve.wait_ge(s_hr, len(CHUNKS) + n + 1)
                link(nc.vector.tensor_reduce(ysum[:, c:c + m], y, AX, ALU.add))
                link(nc.vector.tensor_scalar(ysum[:, c:c + m], ysum[:, c:c + m], -1.0 / C, None, ALU.mult))
                mean = ysum[:, c:c + m].rearrange("p (j o) -> p j o", o=1).broadcast_to([P, m, C])
                nc.vector.tensor_tensor(y, y, mean, ALU.add).then_inc(s_cent, 1)
                if n >= 1:
                    sum_squares(n - 1)
                if n >= 2:
                    invert(n - 2)
            sum_squares(n)
            invert(n - 1)
            invert(n)


_INS = ['x', 'src', 'dst', 'edge_attr_2', 'L0_gnn_W1', 'L0_gnn_root1', 'L0_gnn_b1', 'L0_gnn_W2', 'L0_gnn_root2',
        'L0_gnn_b2']


def kernel(**inputs):
    import numpy as _np
    import concourse.bacc as _bacc
    from concourse import mybir as _mybir
    from concourse.bass_utils import run_bass_kernel_spmd as _run

    nc = _bacc.Bacc("TRN2", target_bir_lowering=False, num_devices=1)
    arrays, args = {}, []
    for name in _INS:
        a = _np.ascontiguousarray(inputs[name])
        arrays[f"in_{name}_dram"] = a
        args.append(nc.dram_tensor(f"in_{name}_dram", a.shape, _mybir.dt.from_np(a.dtype), kind="ExternalInput").ap())
    out = nc.dram_tensor("out_0_dram", (3125, 64), _mybir.dt.float32, kind="ExternalOutput").ap()
    spline_gnn_program(nc, *args, out)
    r = _run(nc, [arrays], core_ids=[0])
    return r.results[0]["out_0_dram"]
```
